# Optimizing a Trainium2 kernel written in Bass

```python
import numpy as np
import jax
import jax.numpy as jnp

def _softmax(x, axis=-1):
    return jax.nn.softmax(x, axis=axis)

def _gelu(x):
    return jax.nn.gelu(x, approximate=True)

def _silu(x):
    return jax.nn.silu(x)

def _sigmoid(x):
    return jax.nn.sigmoid(x)

def _layernorm(x, axis=-1, eps=1e-05):
    m = jnp.mean(x, axis=axis, keepdims=True)
    v = jnp.var(x, axis=axis, keepdims=True)
    return (x - m) / jnp.sqrt(v + eps)

def _scatter_add(tgt, idx, src, axis=0):
    return tgt.at[idx].add(src)

def _segment_sum(src, seg, n):
    return jax.ops.segment_sum(src, seg, n)
kernel_name = 'mk_gnn_preln_d2_gnn_r8_dd7757'

def setup_inputs(seed: int=0):
    np.random.seed(seed)
    _w = jnp.asarray

    def _rec_inputs():
        import jax
        import jax.numpy as jnp
        _gk = jax.random.key(seed)
        x = 0.0001712 + 1 * jax.random.normal(jax.random.fold_in(_gk, 1), (12500, 16), jnp.float32)
        _s = jax.random.randint(jax.random.fold_in(_gk, 2), (200000,), 0, 12500, jnp.int32)
        _d = jax.random.randint(jax.random.fold_in(_gk, 3), (200000,), 0, 12500, jnp.int32)
        _loop = jnp.arange(12500, dtype=jnp.int32)
        src = jnp.concatenate([_s, _d, _loop])
        dst = jnp.concatenate([_d, _s, _loop])
        _o = jnp.argsort(dst, stable=True)
        src = src[_o]
        dst = dst[_o]
        edge_attr_6 = jax.random.uniform(jax.random.fold_in(_gk, 11), (412500, 6), jnp.float32, 0.0, 1)
        edge_attr_8 = 0.000254156 + 0.999948 * jax.random.normal(jax.random.fold_in(_gk, 12), (412500, 8), jnp.float32)
        return (x, src, dst, edge_attr_6, edge_attr_8)
    x, src, dst, edge_attr_6, edge_attr_8 = _rec_inputs()

    def _L0_gnn_setup():
        import jax, jax.numpy as jnp
        import numpy as np
        LATENT = 16
        KDIM = 128
        EDIM = 6
        DEPTH = 4
        N_NODES = 6250
        N_EDGES = 100000

        def _kernel_net(edge_attr, kW1, kb1, kW2, kb2, kW3, kb3):
            h = jax.nn.gelu(edge_attr @ kW1 + kb1)
            h = jax.nn.gelu(h @ kW2 + kb2)
            return h @ kW3 + kb3
        key = jax.random.key(seed)
        ks = jax.random.split(key, 12)
        inp = {'nodes': jax.random.normal(ks[0], (N_NODES, LATENT), dtype=jnp.float32), 'edge_index': jax.random.randint(ks[1], (2, N_EDGES), 0, N_NODES, dtype=jnp.int64), 'edge_attr': jax.random.uniform(ks[2], (N_EDGES, EDIM), dtype=jnp.float32), 'kW1': jax.random.normal(ks[3], (EDIM, KDIM), dtype=jnp.float32) / np.sqrt(EDIM), 'kb1': jnp.zeros((KDIM,), dtype=jnp.float32), 'kW2': jax.random.normal(ks[4], (KDIM, KDIM), dtype=jnp.float32) / np.sqrt(KDIM), 'kb2': jnp.zeros((KDIM,), dtype=jnp.float32), 'kW3': jax.random.normal(ks[5], (KDIM, LATENT * LATENT), dtype=jnp.float32) / np.sqrt(KDIM), 'kb3': jnp.zeros((LATENT * LATENT,), dtype=jnp.float32), 'root_W': jax.random.normal(ks[6], (DEPTH, LATENT, LATENT), dtype=jnp.float32) / np.sqrt(LATENT), 'root_b': jnp.zeros((DEPTH, LATENT), dtype=jnp.float32)}
        return inp
    _L0_gnn_all = _L0_gnn_setup()
    _L0_gnn_in = {k: v for k, v in _L0_gnn_all.items() if k in ('kW1', 'kb1', 'kW2', 'kb2', 'kW3', 'kb3', 'root_W', 'root_b')}
    del _L0_gnn_all

    def _L1_gnn_setup():
        import jax, jax.numpy as jnp
        import numpy as np
        N_NODES = 12500
        N_EDGES = 200000
        IN_C = 16
        OUT_C = 16
        N_EATTR = 8
        key = jax.random.key(seed)
        k1, k2, k3, k4 = jax.random.split(key, 4)
        x = jax.random.normal(k1, (N_NODES, IN_C), dtype=jnp.float32)
        edge_index = jax.random.randint(k2, (2, N_EDGES), 0, N_NODES, dtype=jnp.int64)
        edge_attr = jax.random.normal(k3, (N_EDGES, N_EATTR), dtype=jnp.float32)
        weight_matrix = jax.random.normal(k4, (N_EATTR, OUT_C, IN_C), dtype=jnp.float32) * 0.1
        bias = jnp.zeros((OUT_C,), dtype=jnp.float32)
        return {'x': x, 'edge_index': edge_index, 'edge_attr': edge_attr, 'weight_matrix': weight_matrix, 'bias': bias, 'num_nodes': N_NODES}
    _L1_gnn_all = _L1_gnn_setup()
    _L1_gnn_in = {k: v for k, v in _L1_gnn_all.items() if k in ('weight_matrix', 'bias')}
    del _L1_gnn_all
    return {'x': x, 'src': src, 'dst': dst, 'edge_attr_6': edge_attr_6, 'edge_attr_8': edge_attr_8, 'L0_gnn_kW1': _L0_gnn_in['kW1'], 'L0_gnn_kb1': _L0_gnn_in['kb1'], 'L0_gnn_kW2': _L0_gnn_in['kW2'], 'L0_gnn_kb2': _L0_gnn_in['kb2'], 'L0_gnn_kW3': _L0_gnn_in['kW3'], 'L0_gnn_kb3': _L0_gnn_in['kb3'], 'L0_gnn_root_W': _L0_gnn_in['root_W'], 'L0_gnn_root_b': _L0_gnn_in['root_b'], 'L1_gnn_weight_matrix': _L1_gnn_in['weight_matrix'], 'L1_gnn_bias': _L1_gnn_in['bias']}

def reference(x, src, dst, edge_attr_6, edge_attr_8, L0_gnn_kW1, L0_gnn_kb1, L0_gnn_kW2, L0_gnn_kb2, L0_gnn_kW3, L0_gnn_kb3, L0_gnn_root_W, L0_gnn_root_b, L1_gnn_weight_matrix, L1_gnn_bias):
    import jax
    import jax.numpy as jnp

    def _L0_gnn_ref(nodes, edge_attr, kW1, kb1, kW2, kb2, kW3, kb3, root_W, root_b, edge_index):
        import jax, jax.numpy as jnp
        import numpy as np
        LATENT = 16
        KDIM = 128
        EDIM = 6
        DEPTH = 4
        N_NODES = 6250
        N_EDGES = 100000

        def _kernel_net(edge_attr, kW1, kb1, kW2, kb2, kW3, kb3):
            h = jax.nn.gelu(edge_attr @ kW1 + kb1)
            h = jax.nn.gelu(h @ kW2 + kb2)
            return h @ kW3 + kb3
        src, dst = (edge_index[0], edge_index[1])
        n = nodes.shape[0]
        w = _kernel_net(edge_attr, kW1, kb1, kW2, kb2, kW3, kb3).reshape(-1, LATENT, LATENT)
        deg = jax.ops.segment_sum(jnp.ones((src.shape[0],), nodes.dtype), dst, num_segments=n)
        inv_deg = jnp.where(deg > 0, 1.0 / jnp.maximum(deg, 1.0), 0.0)[:, None]
        for i in range(DEPTH):
            msg = jnp.einsum('ei,eio->eo', nodes[src], w)
            agg = jax.ops.segment_sum(msg, dst, num_segments=n)
            agg = agg * inv_deg
            nodes = jax.nn.gelu(agg + nodes @ root_W[i] + root_b[i])
        return nodes

    def _L1_gnn_ref(x, edge_index, edge_attr, weight_matrix, bias, num_nodes):
        import jax, jax.numpy as jnp
        import numpy as np
        N_NODES = 12500
        N_EDGES = 200000
        IN_C = 16
        OUT_C = 16
        N_EATTR = 8
        src = edge_index[0]
        dst = edge_index[1]
        x_j = x[src]
        msg = jnp.einsum('ea,aoi,ei->eo', edge_attr, weight_matrix, x_j)
        aggr = jax.ops.segment_sum(msg, dst, num_segments=num_nodes)
        return jax.nn.relu(aggr + bias)
    edge_index = jnp.stack([src, dst])
    h = jnp.maximum(_layernorm(x, axis=-1), 0.0)
    x = x + _L0_gnn_ref(h, edge_attr_6, L0_gnn_kW1, L0_gnn_kb1, L0_gnn_kW2, L0_gnn_kb2, L0_gnn_kW3, L0_gnn_kb3, L0_gnn_root_W, L0_gnn_root_b, edge_index)
    h = jnp.maximum(_layernorm(x, axis=-1), 0.0)
    x = x + _L1_gnn_ref(h, edge_index, edge_attr_8, L1_gnn_weight_matrix, L1_gnn_bias, 12500)
    return x

_drawn_inputs = setup_inputs


def setup_inputs(seed=0):
    import zlib

    import numpy as np

    out = dict(_drawn_inputs(seed))
    spreads = {'L0_gnn_kb1': (0.0, 0.519),
     'L0_gnn_kb2': (0.0, 0.347),
     'L0_gnn_kb3': (0.0, 0.1),
     'L0_gnn_root_b': (0.0, 0.1),
     'L1_gnn_bias': (0.0, 2.0)}
    factors = {'edge_attr_6': 5.402}
    for name, (base, spread) in spreads.items():
        noise = np.random.default_rng([zlib.crc32(name.encode()), seed]).standard_normal(out[name].shape)
        drawn = base * np.exp(spread * noise) if base else spread * noise
        out[name] = jnp.asarray(drawn.astype(out[name].dtype))
    for name, factor in factors.items():
        out[name] = (out[name] * factor).astype(out[name].dtype)
    return out
```

```python
import concourse.bass as bass
from concourse import mybir
from contextlib import ExitStack

N = 12500
E = 412500
F = 16
A6, A8 = 6, 8
KD = 128
DEPTH = 4
P = 128
J = -(-N // P)
NP = P * J
QT = 4
QE = QT * P
U = 8
NIT = -(-E // (QE * U))
NQ = NIT * U
NT = NQ * QT
NTP = -(-NT // P) * P
W = 32
R = F + 1
NROW = NP + P
JC = 7
NC = J // JC
JB = JC * F
EPS = 1e-5
FAR = 1 << 20

F32, I32, U32 = mybir.dt.float32, mybir.dt.int32, mybir.dt.uint32
ALU = mybir.AluOpType
ACT = mybir.ActivationFunctionType
AX = mybir.AxisListType


def gnn_program(nc, x, src_q, dst_e, dst_t, attr6, attr8, kW1, kb1, kW2, kb2, kW3, kb3,
                root_W, root_b, Wm, bias, out):
    ctx = ExitStack()
    with ctx:
        def sb(name, shape, dt=F32):
            return ctx.enter_context(nc.sbuf_tensor(name, shape, dt))

        def pb(name, shape):
            return ctx.enter_context(nc.psum_tensor(name, shape, F32))

        def sem(name):
            return ctx.enter_context(nc.semaphore(name))

        table = nc.dram_tensor("table", (NP, 2 * F), F32).ap()
        sums_d = nc.dram_tensor("sums_d", ((DEPTH + 1) * QT * NROW, R), F32).ap()
        base_d = nc.dram_tensor("base_d", (NTP + P,), F32).ap()

        w1 = sb("w1", [A6, KD])
        w2 = sb("w2", [KD, KD])
        w3 = sb("w3", [KD, F * F])
        wm = sb("wm", [A8, F * F])
        b1 = sb("b1", [KD, 1])
        b2 = sb("b2", [KD, 1])
        root_all = sb("root_all", [JB, DEPTH, JB])
        mix = sb("mix", [JB, 2 * JB])
        rootb = sb("rootb", [P, DEPTH, F])
        outb = sb("outb", [P, F])
        ident = sb("ident", [P, P])
        iota = sb("iota", [P, W])
        ones = sb("ones", [P, P])
        rel = sb("rel", [P, NT])
        base_i = sb("base_i", [1, NT], I32)
        idx = sb("idx", [P, U, QT], I32)
        at6 = sb("at6", [A6, U, QE])
        at8 = sb("at8", [A8, U, QE])
        got = sb("got", [P, U, QT, 2 * F])
        h1 = sb("h1", [KD, 2, QE])
        h2 = sb("h2", [KD, 2, QE])
        prod = sb("prod", [P, 2, QT, F, F])
        msg = sb("msg", [P, 2, QT, R])
        hot = sb("hot", [P, 2, QT, W])
        sums = sb("sums", [W, QT, QT, R])
        xs = sb("xs", [P, J, F])
        nodes = sb("nodes", [P, J, F])
        root = sb("root", [P, J, F])
        rows = sb("rows", [P, J, 2 * F])
        agg = sb("agg", [P, QT, J * R])
        tmp = sb("tmp", [P, J, F])
        st = sb("st", [P, 4, J])
        nodeT = sb("nodeT", [JB, 2, P])
        zero = sb("zero", [P, NROW // P * R])
        spare = agg[:, :, :].rearrange("p k n -> p (k n)").bitcast(I32)
        prep_dst = spare[:, 0:NTP].rearrange("p (c e) -> p c e", e=P)
        prep_dt = spare[:, NTP:NTP + NT]
        prep_f = sb("prep_f", [P, NTP // P, P])
        prep_mn = sb("prep_mn", [P, NTP // P])
        prep_bb = sb("prep_bb", [P, NT])
        prep_far = sb("prep_far", [1, NTP + P - NT])

        ph1 = pb("ph1", [P, QE])
        ph2 = pb("ph2", [P, QE])
        pw = [pb(f"pw{b}", [P, QE]) for b in range(4)]
        pwin = [pb(f"pwin{b}", [P, QE]) for b in range(2)]
        pmix = [ph1, ph2]

        s_wt = sem("weights_loaded")
        s_ident0 = sem("identity_cleared")
        s_const = sem("constants_made")
        s_clear = sem("block_diagonals_cleared")
        s_edge = sem("edge_places_loaded")
        s_base = sem("bases_stored")
        s_basefull = sem("bases_reloaded")
        s_dstart = sem("tile_base_ready")
        s_chain = sem("vector_prep_step")
        s_comb = sem("vector_update_step")
        s_x = sem("x_loaded")
        s_rel = sem("rel_ready")
        s_zero = sem("sums_buffers_zeroed")
        s_zsrc = sem("zero_source_made")
        s_idx = [sem(f"idx_loaded{u}") for u in range(U)]
        s_at6 = [sem(f"attr6_loaded{u}") for u in range(U)]
        s_at8 = [sem(f"attr8_loaded{u}") for u in range(U)]
        s_got = [sem(f"rows_gathered{u}") for u in range(U)]
        s_h1 = sem("h1_product_done")
        s_h2 = sem("h2_product_done")
        s_g1 = sem("h1_gelu_done")
        s_g2 = sem("h2_gelu_done")
        s_w = sem("edge_matrices_done")
        s_wfree = sem("edge_matrices_used")
        s_red = sem("products_reduced")
        s_msg = sem("messages_done")
        s_win = sem("window_sums_done")
        s_ev = sem("window_sums_copied")
        s_sfree = sem("window_slots_free")
        s_put = [sem(f"sums_put{k}") for k in range(QT)]
        s_agg = sem("sums_loaded")
        s_var = sem("variance_ready")
        s_std = sem("deviation_ready")
        s_step = sem("update_input_ready")
        s_nodes = sem("nodes_ready")
        s_root = sem("root_matrix_placed")
        s_res = sem("result_ready")
        s_tr = sem("nodes_transposed")
        s_trc = sem("transpose_copied")
        s_mix = sem("mixed")
        s_mixc = sem("mix_copied")
        s_rows = sem("table_rows_ready")
        s_tab = sem("table_stored")
        s_out = sem("out_stored")

        block = ctx.enter_context(nc.Block())

        table_p = table.rearrange("(p j) f -> p j f", p=P)
        x_p = x.rearrange("(p j) f -> p j f", p=P)
        out_p = out.rearrange("(p j) f -> p j f", p=P)
        GL = NQ
        LAST = DEPTH

        def sums_rows(layer, k):
            return sums_d[bass.ds((layer * QT + k) * NROW, NROW), :]

        @block.sync
        def _(sp):
            sp.dma_start(xs[:, :, :], x_p).then_inc(s_x, 16)
            sp.dma_start(prep_dst, dst_e).then_inc(s_edge, 16)
            sp.dma_start(prep_dt, dst_t).then_inc(s_edge, 16)
            sp.wait_ge(s_dstart, 1)
            sp.dma_start(base_d[0:NTP].rearrange("(q c) -> q c", q=P), prep_mn[:, :]).then_inc(s_base, 16)
            sp.wait_ge(s_base, 16)
            sp.dma_start(base_d[NT:NTP + P].rearrange("(a n) -> a n", a=1), prep_far[0:1, 0:NTP + P - NT]).then_inc(s_base, 16)
            sp.wait_ge(s_base, 32)
            sp.dma_start(prep_bb[:, :], base_d[0:NT].rearrange("(a n) -> a n", a=1).to_broadcast([P, NT])).then_inc(s_basefull, 16)
            sp.wait_ge(s_zsrc, 1)
            for k in range(QT):
                sp.dma_start(sums_rows(0, k).rearrange("(p n) r -> p (n r)", p=P), zero[:, :]).then_inc(s_put[k], 16)

            def layer_puts(layer):
                with sp.Fori(0, NIT, 1) as it:
                    for u in range(U):
                        q = it * U + u
                        g = layer * GL + q
                        sp.wait_ge(s_ev, g + 1)
                        for k in range(QT):
                            b = sp.value_load(base_i[0:1, bass.ds(q * QT + k, 1)], min_val=0, max_val=NP - W)
                            sp.wait_ge(s_put[k], (g + 1) * 16)
                            sp.dma_start(sums_d[bass.ds(b + (layer * QT + k) * NROW, W), :],
                                         sums[:, u % QT, k, :]).then_inc(s_put[k], 16)
                        sp.sem_inc(s_sfree, 1)

            def load_sums(layer):
                for k in range(QT):
                    sp.wait_ge(s_put[k], ((layer + 1) * GL + 1) * 16)
                for k in range(QT):
                    sp.dma_start(agg[:, k, :],
                                 sums_d[bass.ds((layer * QT + k) * NROW, NP), :].rearrange("(p j) r -> p (j r)", p=P)
                                 ).then_inc(s_agg, 16)

            def zero_next(layer):
                for k in range(QT):
                    sp.dma_start(sums_rows(layer + 1, k).rearrange("(p n) r -> p (n r)", p=P), zero[:, :]).then_inc(s_zero, 16)

            sp.wait_ge(s_rel, 1)
            with sp.Fori(0, DEPTH, 1) as layer:
                sp.wait_ge(s_rows, layer + 1)
                sp.dma_start(table_p, rows[:, :, :]).then_inc(s_tab, 16)
                zero_next(layer)
                layer_puts(layer)
                sp.wait_ge(s_zero, (layer + 1) * QT * 16)
                load_sums(layer)
            sp.wait_ge(s_rows, LAST + 1)
            sp.dma_start(table_p, rows[:, :, :]).then_inc(s_tab, 16)
            layer_puts(LAST)
            load_sums(LAST)
            sp.wait_ge(s_res, 1)
            sp.dma_start(out_p, tmp[:, :, :]).then_inc(s_out, 16)
            sp.wait_ge(s_out, 16)

        @block.gpsimd
        def _(pool):
            pool.memset(ident[:, :], 0.0).then_inc(s_ident0, 1)
            pool.memset(root_all[:, :, :], 0.0).then_inc(s_clear, 1)
            pool.memset(mix[:, :], 0.0).then_inc(s_clear, 1)
            pool.iota(iota[:, :], pattern=[[1, W]], base=0, channel_multiplier=0,
                      allow_small_or_imprecise_dtypes=True).then_inc(s_const, 1)
            pool.wait_ge(s_ident0, 1)
            pool.affine_select(out=ident[:, :], in_=ident[:, :], compare_op=ALU.not_equal, fill=1.0,
                               base=0, pattern=[[-1, P]], channel_multiplier=1).then_inc(s_const, 1)

            def layer_gathers(layer):
                pool.wait_ge(s_tab, (layer + 1) * 16)
                pool.nop(nofuse=True)
                with pool.Fori(0, NIT, 1) as it:
                    for u in range(U):
                        g = layer * GL + it * U + u
                        pool.wait_ge(s_idx[u], (layer * NIT + it + 1) * 16)
                        pool.wait_ge(s_msg, g + 1)
                        pool.nop(nofuse=True)
                        for k in range(QT):
                            pool.indirect_dma_start(
                                got[:, u, k, :], None, table[:, :],
                                bass.IndirectOffsetOnAxis(ap=idx[:, u, k:k + 1].bitcast(U32), axis=0),
                            ).then_inc(s_got[u], 16)

            with pool.Fori(0, DEPTH, 1) as layer:
                layer_gathers(layer)
            layer_gathers(LAST)

        @block.scalar
        def _(act):
            act.wait_ge(s_clear, 2)
            for dst, srcw in ((w1, kW1), (w2, kW2), (w3, kW3), (wm, Wm)):
                act.dma_start(dst[:, :], srcw).then_inc(s_wt, 16)
            act.dma_start(b1[:, :], kb1.rearrange("(k a) -> k a", a=1)).then_inc(s_wt, 16)
            act.dma_start(b2[:, :], kb2.rearrange("(k a) -> k a", a=1)).then_inc(s_wt, 16)
            act.dma_start(outb[:, :], bias.rearrange("(a f) -> a f", a=1).to_broadcast([P, F])).then_inc(s_wt, 16)
            act.dma_start(rootb[:, :, :], root_b.rearrange("(a d) f -> a d f", a=1).to_broadcast([P, DEPTH, F])).then_inc(s_wt, 16)
            for c in range(JC):
                act.dma_start(root_all[c * F:(c + 1) * F, :, c * F:(c + 1) * F],
                              root_W.rearrange("d i o -> i d o")).then_inc(s_wt, 16)
                act.dma_start(mix[c * F:(c + 1) * F, JB + c * F:JB + (c + 1) * F], kb3).then_inc(s_wt, 16)

            def load_edges(u, q, attr, ring, ring_sem):
                act.dma_start(idx[:, u, :], src_q[bass.ds(q * P, P), :]).then_inc(s_idx[u], 16)
                act.dma_start(ring[:, u, :], attr[:, bass.ds(q * QE, QE)]).then_inc(ring_sem[u], 16)

            for u in range(U):
                load_edges(u, u, attr6, at6, s_at6)
            act.sem_inc(s_sfree, 3)
            act.wait_ge(s_wt, 16 * (8 + 2 * JC))

            def gelu1(n, par):
                act.wait_ge(s_h1, n + 1)
                nc.scalar.activation(h1[:, par, :], ph1[:, :], ACT.Gelu_apprx_tanh, bias=b1[:, 0:1]).then_inc(s_g1, 1)

            def gelu2(n, par):
                act.wait_ge(s_h2, n + 1)
                nc.scalar.activation(h2[:, par, :], ph2[:, :], ACT.Gelu_apprx_tanh, bias=b2[:, 0:1]).then_inc(s_g2, 1)

            def window(g, u):
                act.wait_ge(s_win, g + 1)
                act.wait_ge(s_sfree, g + 1)
                nc.scalar.copy(sums[:, u % QT, :, :],
                               pwin[u % 2][0:W, 0:QT * R].rearrange("w (k r) -> w k r", k=QT)).then_inc(s_ev, 1)

            def deviation(count):
                act.wait_ge(s_var, count)
                nc.scalar.activation(st[:, 2, :], st[:, 1, :], ACT.Sqrt).then_inc(s_std, 1)

            deviation(1)

            def mix_stage(count):
                for c in range(NC):
                    act.wait_ge(s_tr, count + c + 1)
                    nc.scalar.copy(nodeT[:, c % 2, :], pwin[c % 2][0:JB, 0:P]).then_inc(s_trc, 1)

            gelu1(0, 0)
            gelu2(0, 0)
            gelu1(1, 1)
            gelu2(1, 1)
            gelu1(2, 0)
            gelu2(2, 0)
            gelu1(3, 1)
            with act.Fori(0, DEPTH, 1) as layer:
                mix_stage(layer * NC)
                with act.Fori(0, NIT, 1) as it:
                    for u in range(U):
                        g = layer * GL + it * U + u
                        window(g, u)
                        load_edges(u, it * U + u + U, attr6, at6, s_at6)
                        gelu2(g + 3, (u + 3) % 2)
                        gelu1(g + 4, (u + 4) % 2)
                act.wait_ge(s_step, layer + 1)
                nc.scalar.activation(nodes[:, :, :], tmp[:, :, :], ACT.Gelu_apprx_tanh).then_inc(s_nodes, 1)
            for u in range(U):
                act.dma_start(at8[:, u, :], attr8[:, u * QE:(u + 1) * QE]).then_inc(s_at8[u], 16)
            deviation(2)
            with act.Fori(0, NIT, 1) as it:
                for u in range(U):
                    window(LAST * GL + it * U + u, u)
                    load_edges(u, it * U + u + U, attr8, at8, s_at8)
            for u in range(U):
                act.wait_ge(s_idx[u], 16 * ((DEPTH + 1) * NIT + 1))
                act.wait_ge(s_at6[u], 16 * (DEPTH * NIT + 1))
                act.wait_ge(s_at8[u], 16 * (NIT + 1))

        @block.tensor
        def _(pe):
            pe.wait_ge(s_wt, 16 * (8 + 2 * JC))
            pe.wait_ge(s_const, 2)

            def h1_product(n, u, rnd):
                pe.wait_ge(s_at6[u], (rnd + 1) * 16)
                pe.wait_ge(s_g1, n)
                nc.tensor.matmul(ph1[:, :], w1[:, :], at6[:, u, :], start=True, stop=True).then_inc(s_h1, 1)

            def h2_product(n, par):
                pe.wait_ge(s_g1, n + 1)
                nc.tensor.matmul(ph2[:, :], w2[:, :], h1[:, par, :], start=True, stop=True).then_inc(s_h2, 1)

            def edge_matrices(n, u, pair, lhs, rhs):
                bank = pw[u % 2 * 2 + pair]
                pe.wait_ge(s_wfree, n * 2 + pair + 1)
                for t in range(2):
                    k = pair * 2 + t
                    last = nc.tensor.matmul(bank[:, t * F * F:(t + 1) * F * F], lhs[:, k * P:(k + 1) * P], rhs,
                                            start=True, stop=True)
                last.then_inc(s_w, 1)

            def produce(n, u, rnd):
                pe.wait_ge(s_g2, n + 1)
                h2_product(n + 1, (u + 1) % 2)
                edge_matrices(n, u, 0, h2[:, u % 2, :], w3[:, :])
                u1 = (u + 2) % U
                h1_product(n + 2, u1, rnd + (u + 2) // U)
                edge_matrices(n, u, 1, h2[:, u % 2, :], w3[:, :])

            def window(g, u):
                pe.wait_ge(s_msg, g + 1 + U)
                for k in range(QT):
                    last = nc.tensor.matmul(pwin[u % 2][0:W, k * R:(k + 1) * R], hot[:, u % 2, k, :],
                                            msg[:, u % 2, k, :], start=True, stop=True)
                last.then_inc(s_win, 1)

            def mix_stage(layer):
                pe.wait_ge(s_nodes, layer + 1)
                for c in range(NC):
                    if c >= 2:
                        pe.wait_ge(s_trc, layer * NC + c - 1)
                    nc.tensor.transpose(pwin[c % 2][0:JB, 0:P],
                                        nodes[:, c * JC:(c + 1) * JC, :].rearrange("p j f -> p (j f)"),
                                        ident[:, :]).then_inc(s_tr, 1)
                    pe.wait_ge(s_trc, layer * NC + c + 1)
                    if c == 0:
                        pe.wait_ge(s_root, layer + 1)
                    if c >= 2:
                        pe.wait_ge(s_mixc, layer * NC + c - 1)
                    nc.tensor.matmul(pmix[c % 2][:, 0:2 * JB], nodeT[:, c % 2, :], mix[:, :],
                                     start=True, stop=True).then_inc(s_mix, 1)
                pe.wait_ge(s_mixc, (layer + 1) * NC)
                pe.nop(nofuse=True)

            pe.wait_ge(s_at6[0], 16)
            nc.tensor.matmul(ph1[:, :], w1[:, :], at6[:, 0, :], start=True, stop=True).then_inc(s_h1, 1)
            h2_product(0, 0)
            h1_product(1, 1, 0)
            produce(0, 0, 0)
            produce(1, 1, 0)
            pe.wait_ge(s_g1, 4)
            pe.wait_ge(s_g2, 3)
            with pe.Fori(0, DEPTH, 1) as layer:
                mix_stage(layer)
                with pe.Fori(0, NIT, 1) as it:
                    for u in range(U):
                        g = layer * GL + it * U + u
                        window(g, u)
                        v = (u + 2) % U
                        produce(g + 2, v, layer * NIT + it + (u + 2) // U)
            for u in range(2):
                for pair in range(2):
                    pe.wait_ge(s_at8[u], 16)
                    edge_matrices(LAST * GL + 2 + u, u, pair, at8[:, u, :], wm[:, :])
            with pe.Fori(0, NIT, 1) as it:
                for u in range(U):
                    g = LAST * GL + it * U + u
                    pe.wait_ge(s_ev, g - 1)
                    window(g, u)
                    v = (u + 2) % U
                    pe.wait_ge(s_at8[v], (it + (u + 2) // U + 1) * 16)
                    for pair in range(2):
                        edge_matrices(g + 4, v, pair, at8[:, v, :], wm[:, :])

        @block.vector
        def _(dve):
            chain = [0]

            def link(ins):
                chain[0] += 1
                ins.then_inc(s_chain, 1)
                dve.wait_ge(s_chain, chain[0])

            dve.sem_inc(s_msg, U)
            dve.sem_inc(s_wfree, 4)
            dve.memset(msg[:, :, :, :], 1.0)
            dve.memset(prep_far[:, :], float(FAR))
            dve.memset(zero[:, :], 0.0).then_inc(s_zsrc, 1)
            dve.wait_ge(s_edge, 32)
            link(nc.vector.tensor_copy(prep_f[:, :, :], prep_dst))
            nc.vector.tensor_reduce(prep_mn[:, :], prep_f[:, :, :], axis=AX.X, op=ALU.min).then_inc(s_dstart, 1)
            link(nc.vector.tensor_copy(rel[:, :], prep_dt))
            dve.wait_ge(s_basefull, 16)
            link(nc.vector.tensor_tensor(rel[:, :], rel[:, :], prep_bb[:, :], ALU.subtract))
            nc.vector.tensor_copy(base_i[0:1, :], prep_bb[0:1, :]).then_inc(s_rel, 1)

            def norm(ready):
                link(nc.vector.tensor_reduce(st[:, 0, :], xs[:, :, :], axis=AX.X, op=ALU.add))
                link(nc.vector.tensor_scalar(st[:, 0, :], st[:, 0, :], 1.0 / F, None, ALU.mult))
                link(nc.vector.tensor_tensor(tmp[:, :, :], xs[:, :, :],
                                             st[:, 0, :].unsqueeze(2).to_broadcast([P, J, F]), ALU.subtract))
                link(nc.vector.tensor_tensor(nodes[:, :, :], tmp[:, :, :], tmp[:, :, :], ALU.mult))
                link(nc.vector.tensor_reduce(st[:, 1, :], nodes[:, :, :], axis=AX.X, op=ALU.add))
                nc.vector.tensor_scalar(st[:, 1, :], st[:, 1, :], 1.0 / F, EPS, ALU.mult, ALU.add).then_inc(s_var, 1)
                dve.wait_ge(s_std, ready)
                link(nc.vector.reciprocal(st[:, 3, :], st[:, 2, :]))
                link(nc.vector.tensor_tensor(nodes[:, :, :], tmp[:, :, :],
                                             st[:, 3, :].unsqueeze(2).to_broadcast([P, J, F]), ALU.mult))

            dve.wait_ge(s_x, 16)
            norm(1)
            nc.vector.tensor_scalar(nodes[:, :, :], nodes[:, :, :], 0.0, None, ALU.max).then_inc(s_nodes, 1)
            dve.wait_ge(s_wt, 16 * (8 + 2 * JC))
            dve.wait_ge(s_const, 2)

            def quad(g, q, u, rnd, ahead, with_y):
                s = u % 2
                dve.wait_ge(s_got[u], (rnd + 1) * 16 * QT)
                for pair in range(2):
                    dve.wait_ge(s_w, (g + ahead) * 2 + pair + 1)
                    nc.vector.tensor_tensor(
                        prod[:, s, pair * 2:pair * 2 + 2, :, :],
                        pw[s * 2 + pair][:, :].rearrange("p (t o i) -> p t o i", t=2, o=F),
                        got[:, u, pair * 2:pair * 2 + 2, F:2 * F].unsqueeze(2).to_broadcast([P, 2, F, F]),
                        ALU.mult).then_inc(s_wfree, 1)
                    if pair == 0:
                        nc.vector.tensor_tensor(
                            hot[:, s, :, :], iota[:, :].unsqueeze(1).to_broadcast([P, QT, W]),
                            rel[:, bass.ds(q * QT, QT)].unsqueeze(2).to_broadcast([P, QT, W]), ALU.is_equal)
                dve.wait_ge(s_wfree, (g + ahead) * 2 + 2 + 4)
                red = nc.vector.tensor_reduce(
                    msg[:, s, :, 0:F], prod[:, s, :, :, :].rearrange("p t o i -> p (t o) i"), axis=AX.X, op=ALU.add)
                if with_y:
                    red.then_inc(s_red, 1)
                    dve.wait_ge(s_red, g + 1)
                    nc.vector.tensor_tensor(msg[:, s, :, 0:F], msg[:, s, :, 0:F], got[:, u, :, 0:F],
                                            ALU.add).then_inc(s_msg, 1)
                else:
                    red.then_inc(s_msg, 1)

            def combine(layer):
                c = [0]
                def own(ins):
                    c[0] += 1
                    ins.then_inc(s_comb, 1)
                    dve.wait_ge(s_comb, layer * 6 + c[0])
                dve.wait_ge(s_agg, (layer + 1) * QT * 16)
                nc.vector.tensor_tensor(agg[:, 0, :], agg[:, 0, :], agg[:, 1, :], ALU.add)
                own(nc.vector.tensor_tensor(agg[:, 2, :], agg[:, 2, :], agg[:, 3, :], ALU.add))
                own(nc.vector.tensor_tensor(agg[:, 0, :], agg[:, 0, :], agg[:, 2, :], ALU.add))
                a = agg[:, 0, :].rearrange("p (j r) -> p j r", r=R)
                return a, own

            with dve.Fori(0, DEPTH, 1) as layer:
                nc.vector.tensor_copy(mix[:, 0:JB], root_all[:, bass.ds(layer, 1), :].rearrange("k a n -> k (a n)")).then_inc(s_root, 1)
                for c in range(NC):
                    dve.wait_ge(s_mix, layer * NC + c + 1)
                    half = pmix[c % 2][:, 0:2 * JB]
                    nc.vector.tensor_tensor(root[:, c * JC:(c + 1) * JC, :],
                                            half[:, 0:JB].rearrange("p (j f) -> p j f", f=F),
                                            rootb[:, bass.ds(layer, 1), :].to_broadcast([P, JC, F]), ALU.add)
                    nc.vector.tensor_copy(rows[:, c * JC:(c + 1) * JC, 0:F],
                                          half[:, JB:2 * JB].rearrange("p (j f) -> p j f", f=F)).then_inc(s_mixc, 1)
                nc.vector.tensor_copy(rows[:, :, F:2 * F], nodes[:, :, :]).then_inc(s_rows, 1)
                with dve.Fori(0, NIT, 1) as it:
                    for u in range(U):
                        q = it * U + u
                        quad(layer * GL + q, q, u, layer * NIT + it, 0, True)
                a, own = combine(layer)
                deg = a[:, :, F]
                nc.vector.tensor_scalar(st[:, 1, :], deg, 0.0, None, ALU.is_gt)
                own(nc.vector.tensor_scalar(st[:, 0, :], deg, 1.0, None, ALU.max))
                own(nc.vector.reciprocal(st[:, 2, :], st[:, 0, :]))
                own(nc.vector.tensor_tensor(st[:, 3, :], st[:, 2, :], st[:, 1, :], ALU.mult))
                own(nc.vector.tensor_tensor(tmp[:, :, :], a[:, :, 0:F],
                                            st[:, 3, :].unsqueeze(2).to_broadcast([P, J, F]), ALU.mult))
                nc.vector.tensor_tensor(tmp[:, :, :], tmp[:, :, :], root[:, :, :], ALU.add).then_inc(s_step, 1)
                dve.wait_ge(s_nodes, layer + 2)
            dve.sem_inc(s_wfree, 4)
            link(nc.vector.tensor_tensor(xs[:, :, :], xs[:, :, :], nodes[:, :, :], ALU.add))
            norm(2)
            nc.vector.tensor_scalar(rows[:, :, F:2 * F], nodes[:, :, :], 0.0, None, ALU.max).then_inc(s_rows, 1)
            with dve.Fori(0, NIT, 1) as it:
                for u in range(U):
                    q = it * U + u
                    quad(LAST * GL + q, q, u, LAST * NIT + it, 2, False)
            a, own = combine(LAST)
            link(nc.vector.tensor_tensor(tmp[:, :, :], a[:, :, 0:F],
                                         outb[:, :].unsqueeze(1).to_broadcast([P, J, F]), ALU.add))
            link(nc.vector.tensor_scalar(tmp[:, :, :], tmp[:, :, :], 0.0, None, ALU.max))
            nc.vector.tensor_tensor(tmp[:, :, :], tmp[:, :, :], xs[:, :, :], ALU.add).then_inc(s_res, 1)


_OUT = ("out", (NP, F))


def kernel(**inputs):
    import numpy as np
    import concourse.bacc as bacc
    from concourse.bass_utils import run_bass_kernel_spmd

    a = {k: np.ascontiguousarray(v) for k, v in inputs.items()}

    def padded(v, n, fill=0):
        more = np.full((n - v.shape[0],) + v.shape[1:], fill, v.dtype)
        return np.concatenate([v, more])

    def turned(v):
        return np.concatenate([v, v[:U]])

    src = padded(a["src"].astype(np.int32, copy=False), NT * P)
    dst = padded(a["dst"].astype(np.int32, copy=False), NTP * P, N)
    src_q = turned(src.reshape(NQ, QT, P).transpose(0, 2, 1)).reshape(-1, QT)

    def attributes(v):
        v = turned(padded(v, NQ * QE).reshape(NQ, QE, -1))
        return v.reshape(-1, v.shape[-1]).T

    arrays = {
        "x": padded(a["x"], NP),
        "src_q": src_q,
        "dst_e": dst.reshape(P, NTP // P, P),
        "dst_t": dst[:NT * P].reshape(NT, P).T,
        "attr6": attributes(a["edge_attr_6"]),
        "attr8": attributes(a["edge_attr_8"]),
        "kW1": a["L0_gnn_kW1"], "kb1": a["L0_gnn_kb1"],
        "kW2": a["L0_gnn_kW2"], "kb2": a["L0_gnn_kb2"],
        "kW3": a["L0_gnn_kW3"].reshape(KD, F, F).transpose(0, 2, 1).reshape(KD, F * F),
        "kb3": a["L0_gnn_kb3"].reshape(F, F),
        "root_W": a["L0_gnn_root_W"], "root_b": a["L0_gnn_root_b"],
        "Wm": a["L1_gnn_weight_matrix"].reshape(A8, F * F), "bias": a["L1_gnn_bias"],
    }
    arrays = {k: np.ascontiguousarray(v) for k, v in arrays.items()}
    nc = bacc.Bacc("TRN2", target_bir_lowering=False, num_devices=1)
    args = [nc.dram_tensor("in_" + k, v.shape, mybir.dt.from_np(v.dtype), kind="ExternalInput").ap()
            for k, v in arrays.items()]
    args.append(nc.dram_tensor(_OUT[0], _OUT[1], F32, kind="ExternalOutput").ap())
    gnn_program(nc, *args)
    r = run_bass_kernel_spmd(nc, [{"in_" + k: v for k, v in arrays.items()}], core_ids=[0])
    return r.results[0][_OUT[0]][:N]
```

```python
import concourse.bass as bass
from concourse import mybir
from contextlib import ExitStack

N = 12500
E = 412500
F = 16
A6, A8 = 6, 8
A8P = 32
KD = 128
DEPTH = 4
P = 128
J = -(-N // P)
NP = P * J
QT = 4
QE = QT * P
U = 8
NIT = -(-E // (QE * U))
NQ = NIT * U
NT = NQ * QT
QC = -(-NQ // P)
NQP = P * QC
W = 32
B = 2
R = F + 1
NROW = NP + P
JC = 7
NC = J // JC
JB = JC * F
EPS = 1e-5
FAR = 1 << 20

F32, I32, U32 = mybir.dt.float32, mybir.dt.int32, mybir.dt.uint32
ALU = mybir.AluOpType
ACT = mybir.ActivationFunctionType
AX = mybir.AxisListType


def gnn_program(nc, x, src_q, dst_e, dst_t, attr6, attr8, kW1, kb1, kW2, kb2, kW3, kb3,
                root_W, root_b, Wm, bias, out):
    ctx = ExitStack()
    with ctx:
        def sb(name, shape, dt=F32):
            return ctx.enter_context(nc.sbuf_tensor(name, shape, dt))

        def pb(name, shape):
            return ctx.enter_context(nc.psum_tensor(name, shape, F32))

        def sem(name):
            return ctx.enter_context(nc.semaphore(name))

        table = nc.dram_tensor("table", (NP, 2 * F), F32).ap()
        sums_d = nc.dram_tensor("sums_d", ((DEPTH + 1) * B * NROW, R), F32).ap()
        base_d = nc.dram_tensor("base_d", (NQP + B,), F32).ap()

        w1 = sb("w1", [A6, KD])
        w2 = sb("w2", [KD, KD])
        w3 = sb("w3", [KD, F * F])
        wm = sb("wm", [A8P + A8, F * F])[A8P:A8P + A8, :]
        b1 = sb("b1", [KD, 1])
        b2 = sb("b2", [KD, 1])
        root_all = sb("root_all", [JB, DEPTH, JB])
        mix = sb("mix", [JB, 2 * JB])
        rootb = sb("rootb", [P, DEPTH, F])
        outb = sb("outb", [P, F])
        ident = sb("ident", [P, P])
        iota = sb("iota", [P, W])
        ones = sb("ones", [P, P])
        rel = sb("rel", [P, NT])
        base_i = sb("base_i", [1, NQ], I32)
        flag = sb("flag", [P, 1], I32)
        idx = sb("idx", [P, U, QT], I32)
        attr = sb("attr", [A8P + A8, U, QE])
        at6 = attr[0:A6, :, :]
        at8 = attr[A8P:A8P + A8, :, :]
        got = sb("got", [P, U, QT, 2 * F])
        h1 = sb("h1", [KD, 2, QE])
        h2 = sb("h2", [KD, 2, QE])
        prod = sb("prod", [P, 2, QT, F, F])
        msg = sb("msg", [P, 2, QT, R])
        hot = sb("hot", [P, 2, QT, W])
        sums = sb("sums", [W, 4, R])
        xs = sb("xs", [P, J, F])
        nodes = sb("nodes", [P, J, F])
        root = sb("root", [P, J, F])
        rows = sb("rows", [P, J, 2 * F])
        agg = sb("agg", [P, B, J * R])
        tmp = sb("tmp", [P, J, F])
        st = sb("st", [P, 4, J])
        nodeT = sb("nodeT", [JB, 2, P])
        zero = sb("zero", [P, NROW // P * R])
        spare = agg[:, :, :].rearrange("p k n -> p (k n)").bitcast(I32)
        prep_dt = spare[:, 0:NT]
        prep_dst = sb("prep_dst", [P, QC, QE], I32)
        prep_f = sb("prep_f", [P, QC, QE])
        prep_m = sb("prep_m", [P, 6, QC])
        prep_bb = sb("prep_bb", [P, NQ])
        prep_far = sb("prep_far", [1, NQP + B - NQ])
        dst_f = sb("dst_f", [P, NT])
        row_i = sb("row_i", [P, QT, P], I32)
        row_f = sb("row_f", [P, QT, P])
        below = sb("below", [P, P])
        same = sb("same", [P, 2, QT, P])
        dup = sb("dup", [P, QT, P])
        spot = sb("spot", [P, 4, QT])
        first_row = sb("first_row", [P, 1])
        spill = sb("spill", [P, 1])
        get_i = sb("get_i", [P, QT], I32)
        put_i = sb("put_i", [P, QT], I32)
        gsum = sb("gsum", [P, 4, QT, R])
        cur = sb("cur", [P, QT, R])

        ph1 = pb("ph1", [P, QE])
        ph2 = pb("ph2", [P, QE])
        pw = [pb(f"pw{b}", [P, QE]) for b in range(4)]
        pwin = [pb(f"pwin{b}", [P, QE]) for b in range(2)]
        pmix = [ph1, ph2]

        s_wt = sem("weights_loaded")
        s_ident0 = sem("identity_cleared")
        s_const = sem("constants_made")
        s_clear = sem("block_diagonals_cleared")
        s_edge = sem("edge_places_loaded")
        s_base = sem("bases_stored")
        s_basefull = sem("bases_reloaded")
        s_dstart = sem("quad_base_ready")
        s_fit = sem("misfits_counted")
        s_fitsum = sem("misfits_summed")
        s_flag = sem("flag_ready")
        s_row = sem("dst_row_loaded")
        s_gen = sem("general_step")
        s_cur = sem("general_rows_gathered")
        s_add = sem("general_rows_added")
        s_back = sem("general_rows_scattered")
        s_chain = sem("vector_prep_step")
        s_comb = sem("vector_update_step")
        s_x = sem("x_loaded")
        s_rel = sem("rel_ready")
        s_zero = sem("sums_buffers_zeroed")
        s_zsrc = sem("zero_source_made")
        s_idx = [sem(f"idx_loaded{u}") for u in range(U)]
        s_at6 = [sem(f"attr6_loaded{u}") for u in range(U)]
        s_at8 = [sem(f"attr8_loaded{u}") for u in range(U)]
        s_got = [sem(f"rows_gathered{u}") for u in range(U)]
        s_h1 = sem("h1_product_done")
        s_h2 = sem("h2_product_done")
        s_g1 = sem("h1_gelu_done")
        s_g2 = sem("h2_gelu_done")
        s_w = sem("edge_matrices_done")
        s_wfree = sem("edge_matrices_used")
        s_red = sem("products_reduced")
        s_msg = sem("messages_done")
        s_win = sem("window_sums_done")
        s_ev = sem("window_sums_copied")
        s_sfree = sem("window_slots_free")
        s_put = [sem(f"sums_put{m}") for m in range(B)]
        s_agg = sem("sums_loaded")
        s_var = sem("variance_ready")
        s_std = sem("deviation_ready")
        s_step = sem("update_input_ready")
        s_nodes = sem("nodes_ready")
        s_root = sem("root_matrix_placed")
        s_res = sem("result_ready")
        s_tr = sem("nodes_transposed")
        s_trc = sem("transpose_copied")
        s_mix = sem("mixed")
        s_mixc = sem("mix_copied")
        s_rows = sem("table_rows_ready")
        s_tab = sem("table_stored")
        s_out = sem("out_stored")

        block = ctx.enter_context(nc.Block())

        table_p = table.rearrange("(p j) f -> p j f", p=P)
        x_p = x.rearrange("(p j) f -> p j f", p=P)
        out_p = out.rearrange("(p j) f -> p j f", p=P)
        GL = NQ
        LAST = DEPTH

        def sums_rows(layer, m, n):
            return sums_d[bass.ds((layer * B + m) * NROW, n), :].rearrange("(p j) r -> p (j r)", p=P)

        @block.sync
        def _(sp):
            sp.dma_start(xs[:, :, :], x_p).then_inc(s_x, 16)
            sp.dma_start(prep_dst[:, :, :], dst_e).then_inc(s_edge, 16)
            sp.dma_start(prep_dt, dst_t).then_inc(s_edge, 16)
            sp.wait_ge(s_zsrc, 1)
            for layer in range(DEPTH + 1):
                for m in range(B):
                    sp.dma_start(sums_rows(layer, m, NROW), zero[:, :]).then_inc(s_zero if layer else s_put[m], 16)
            sp.wait_ge(s_dstart, 1)
            sp.dma_start(base_d[0:NQP].rearrange("(p c) -> p c", p=P), prep_m[:, 0, :]).then_inc(s_base, 16)
            sp.wait_ge(s_base, 16)
            sp.dma_start(base_d[NQ:NQP + B].rearrange("(a n) -> a n", a=1), prep_far[0:1, :]).then_inc(s_base, 16)
            sp.wait_ge(s_base, 32)
            sp.dma_start(prep_bb[:, :], base_d[0:NQ].rearrange("(a n) -> a n", a=1).to_broadcast([P, NQ])
                         ).then_inc(s_basefull, 16)
            for m in range(B):
                sp.dma_start(prep_m[:, 2 + m, :], base_d[1 + m:1 + m + NQP].rearrange("(p c) -> p c", p=P)
                             ).then_inc(s_basefull, 16)

            def place_windows(layer):
                with sp.Fori(0, NIT, 1) as it:
                    for u in range(U):
                        q = it * U + u
                        g = layer * GL + q
                        m = u % B
                        base = sp.value_load(base_i[0:1, bass.ds(q, 1)], min_val=0, max_val=NP - W)
                        sp.wait_ge(s_ev, g + 1)
                        sp.wait_ge(s_put[m], (layer * (GL // B) + it * (U // B) + (u // B + 1)) * 16)
                        sp.dma_start(sums_d[bass.ds(base + (layer * B + m) * NROW, W), :],
                                     sums[:, u % 4, :]).then_inc(s_put[m], 16)
                        sp.sem_inc(s_sfree, 1)

            def dst_rows(layer):
                with sp.Fori(0, NIT, 1) as it:
                    for u in range(U):
                        g = layer * GL + it * U + u
                        sp.wait_ge(s_msg, g + U)
                        sp.dma_start(row_i[:, :, :].rearrange("p t e -> p (t e)"),
                                     dst_e.rearrange("p c e -> (p c) e")[bass.ds(it * U + u, 1), :].to_broadcast([P, QE])
                                     ).then_inc(s_row, 16)

            def load_sums(layer, general):
                if general:
                    sp.wait_ge(s_back, (layer + 1) * (GL * QT * 16))
                    sp.wait_ge(s_put[1], 16)
                else:
                    for m in range(B):
                        sp.wait_ge(s_put[m], ((layer + 1) * (GL // B) + 1) * 16)
                for m in range(B):
                    sp.dma_start(agg[:, m, :], sums_rows(layer, m, NP)).then_inc(s_agg, 16)

            def layers(general):
                add_up = dst_rows if general else place_windows
                with sp.Fori(0, DEPTH, 1) as layer:
                    sp.wait_ge(s_rows, layer + 1)
                    sp.dma_start(table_p, rows[:, :, :]).then_inc(s_tab, 16)
                    add_up(layer)
                    load_sums(layer, general)
                sp.wait_ge(s_rows, LAST + 1)
                sp.dma_start(table_p, rows[:, :, :]).then_inc(s_tab, 16)
                add_up(LAST)
                load_sums(LAST, general)

            sp.wait_ge(s_zero, DEPTH * B * 16)
            sp.wait_ge(s_flag, 1)
            misfits = sp.value_load(flag[0:1, 0:1], min_val=0, max_val=1)
            with sp.If(misfits == 0):
                layers(False)
            with sp.Else():
                layers(True)
            sp.wait_ge(s_res, 1)
            sp.dma_start(out_p, tmp[:, :, :]).then_inc(s_out, 16)
            sp.wait_ge(s_out, 16)

        @block.gpsimd
        def _(pool):
            pool.memset(ident[:, :], 0.0).then_inc(s_ident0, 1)
            pool.memset(root_all[:, :, :], 0.0).then_inc(s_clear, 1)
            pool.memset(mix[:, :], 0.0).then_inc(s_clear, 1)
            pool.iota(iota[:, :], pattern=[[1, W]], base=0, channel_multiplier=0,
                      allow_small_or_imprecise_dtypes=True).then_inc(s_const, 1)
            pool.wait_ge(s_ident0, 1)
            pool.affine_select(out=ident[:, :], in_=ident[:, :], compare_op=ALU.not_equal, fill=1.0,
                               base=0, pattern=[[-1, P]], channel_multiplier=1).then_inc(s_const, 1)

            pool.memset(ones[:, :], 1.0).then_inc(s_const, 1)
            pool.memset(below[:, :], 1.0).then_inc(s_ident0, 1)
            pool.wait_ge(s_ident0, 2)
            pool.affine_select(out=below[:, :], in_=below[:, :], compare_op=ALU.is_ge, fill=0.0,
                               base=-1, pattern=[[-1, P]], channel_multiplier=1).then_inc(s_const, 1)
            pool.iota(spill[:, :], pattern=[[1, 1]], base=NP, channel_multiplier=1,
                      allow_small_or_imprecise_dtypes=True).then_inc(s_const, 1)

            def add_rows(g, u):
                pool.wait_ge(s_ev, g + 1)
                for k in range(QT):
                    n = g * QT + k
                    pool.nop(nofuse=True)
                    pool.indirect_dma_start(
                        cur[:, k, :], None, sums_d[:, :],
                        bass.IndirectOffsetOnAxis(ap=get_i[:, k:k + 1].bitcast(U32), axis=0)).then_inc(s_cur, 16)
                    pool.wait_ge(s_cur, n * 16 + 16)
                    pool.tensor_tensor(cur[:, k, :], cur[:, k, :], gsum[:, u % 4, k, :], ALU.add).then_inc(s_add, 1)
                    pool.wait_ge(s_add, n + 1)
                    pool.nop(nofuse=True)
                    pool.indirect_dma_start(
                        sums_d[:, :], bass.IndirectOffsetOnAxis(ap=put_i[:, k:k + 1].bitcast(U32), axis=0),
                        cur[:, k, :], None).then_inc(s_back, 16)
                    pool.wait_ge(s_back, n * 16 + 16)
                pool.sem_inc(s_sfree, 1)

            def layer_gathers(layer, general):
                pool.wait_ge(s_tab, (layer + 1) * 16)
                pool.nop(nofuse=True)
                with pool.Fori(0, NIT, 1) as it:
                    for u in range(U):
                        g = layer * GL + it * U + u
                        pool.wait_ge(s_idx[u], (layer * NIT + it + 1) * 16)
                        pool.wait_ge(s_msg, g + 1)
                        pool.nop(nofuse=True)
                        for k in range(QT):
                            pool.indirect_dma_start(
                                got[:, u, k, :], None, table[:, :],
                                bass.IndirectOffsetOnAxis(ap=idx[:, u, k:k + 1].bitcast(U32), axis=0),
                            ).then_inc(s_got[u], 16)
                        if general:
                            add_rows(g, u)

            def layers(general):
                with pool.Fori(0, DEPTH, 1) as layer:
                    layer_gathers(layer, general)
                layer_gathers(LAST, general)

            pool.wait_ge(s_flag, 1)
            misfits = pool.value_load(flag[0:1, 0:1], min_val=0, max_val=1)
            with pool.If(misfits == 0):
                layers(False)
            with pool.Else():
                for m in range(B):
                    pool.wait_ge(s_put[m], 16)
                pool.wait_ge(s_zero, DEPTH * B * 16)
                layers(True)

        @block.scalar
        def _(act):
            act.wait_ge(s_clear, 2)
            for dst, srcw in ((w1, kW1), (w2, kW2), (w3, kW3), (wm, Wm)):
                act.dma_start(dst[:, :], srcw).then_inc(s_wt, 16)
            act.dma_start(b1[:, :], kb1.rearrange("(k a) -> k a", a=1)).then_inc(s_wt, 16)
            act.dma_start(b2[:, :], kb2.rearrange("(k a) -> k a", a=1)).then_inc(s_wt, 16)
            act.dma_start(outb[:, :], bias.rearrange("(a f) -> a f", a=1).to_broadcast([P, F])).then_inc(s_wt, 16)
            act.dma_start(rootb[:, :, :], root_b.rearrange("(a d) f -> a d f", a=1).to_broadcast([P, DEPTH, F])).then_inc(s_wt, 16)
            for c in range(JC):
                act.dma_start(root_all[c * F:(c + 1) * F, :, c * F:(c + 1) * F],
                              root_W.rearrange("d i o -> i d o")).then_inc(s_wt, 16)
                act.dma_start(mix[c * F:(c + 1) * F, JB + c * F:JB + (c + 1) * F], kb3).then_inc(s_wt, 16)

            def load_edges(u, q, attr, ring, ring_sem):
                act.dma_start(idx[:, u, :], src_q[bass.ds(q * P, P), :]).then_inc(s_idx[u], 16)
                act.dma_start(ring[:, u, :], attr[:, bass.ds(q * QE, QE)]).then_inc(ring_sem[u], 16)

            for u in range(U):
                load_edges(u, u, attr6, at6, s_at6)
            act.sem_inc(s_sfree, 2)
            act.wait_ge(s_wt, 16 * (8 + 2 * JC))

            def gelu1(n, par):
                act.wait_ge(s_h1, n + 1)
                nc.scalar.activation(h1[:, par, :], ph1[:, :], ACT.Gelu_apprx_tanh, bias=b1[:, 0:1]).then_inc(s_g1, 1)

            def gelu2(n, par):
                act.wait_ge(s_h2, n + 1)
                nc.scalar.activation(h2[:, par, :], ph2[:, :], ACT.Gelu_apprx_tanh, bias=b2[:, 0:1]).then_inc(s_g2, 1)

            def window(g, u, general):
                act.wait_ge(s_win, g + 1)
                act.wait_ge(s_sfree, g + 1)
                if general:
                    nc.scalar.copy(gsum[:, u % 4, :, :],
                                   pwin[u % 2][:, 0:QT * R].rearrange("p (k r) -> p k r", k=QT)).then_inc(s_ev, 1)
                else:
                    nc.scalar.copy(sums[:, u % 4, :], pwin[u % 2][0:W, 0:R]).then_inc(s_ev, 1)

            def deviation(count):
                act.wait_ge(s_var, count)
                nc.scalar.activation(st[:, 2, :], st[:, 1, :], ACT.Sqrt).then_inc(s_std, 1)

            deviation(1)

            def mix_stage(count):
                for c in range(NC):
                    act.wait_ge(s_tr, count + c + 1)
                    nc.scalar.copy(nodeT[:, c % 2, :], pwin[c % 2][0:JB, 0:P]).then_inc(s_trc, 1)

            gelu1(0, 0)
            gelu2(0, 0)
            gelu1(1, 1)
            gelu2(1, 1)
            gelu1(2, 0)
            gelu2(2, 0)
            gelu1(3, 1)
            def layers(general):
                with act.Fori(0, DEPTH, 1) as layer:
                    mix_stage(layer * NC)
                    with act.Fori(0, NIT, 1) as it:
                        for u in range(U):
                            g = layer * GL + it * U + u
                            window(g, u, general)
                            load_edges(u, it * U + u + U, attr6, at6, s_at6)
                            gelu2(g + 3, (u + 3) % 2)
                            gelu1(g + 4, (u + 4) % 2)
                    act.wait_ge(s_step, layer + 1)
                    nc.scalar.activation(nodes[:, :, :], tmp[:, :, :], ACT.Gelu_apprx_tanh).then_inc(s_nodes, 1)
                for u in range(U):
                    act.dma_start(at8[:, u, :], attr8[:, u * QE:(u + 1) * QE]).then_inc(s_at8[u], 16)
                deviation(2)
                with act.Fori(0, NIT, 1) as it:
                    for u in range(U):
                        window(LAST * GL + it * U + u, u, general)
                        load_edges(u, it * U + u + U, attr8, at8, s_at8)

            act.wait_ge(s_flag, 1)
            misfits = act.value_load(flag[0:1, 0:1], min_val=0, max_val=1)
            with act.If(misfits == 0):
                layers(False)
            with act.Else():
                layers(True)
            for u in range(U):
                act.wait_ge(s_idx[u], 16 * ((DEPTH + 1) * NIT + 1))
                act.wait_ge(s_at6[u], 16 * (DEPTH * NIT + 1))
                act.wait_ge(s_at8[u], 16 * (NIT + 1))

        @block.tensor
        def _(pe):
            pe.wait_ge(s_wt, 16 * (8 + 2 * JC))
            pe.wait_ge(s_const, 5)

            def h1_product(n, u, rnd):
                pe.wait_ge(s_at6[u], (rnd + 1) * 16)
                pe.wait_ge(s_g1, n)
                nc.tensor.matmul(ph1[:, :], w1[:, :], at6[:, u, :], start=True, stop=True).then_inc(s_h1, 1)

            def h2_product(n, par):
                pe.wait_ge(s_g1, n + 1)
                nc.tensor.matmul(ph2[:, :], w2[:, :], h1[:, par, :], start=True, stop=True).then_inc(s_h2, 1)

            def edge_matrices(n, u, pair, lhs, rhs):
                bank = pw[u % 2 * 2 + pair]
                pe.wait_ge(s_wfree, n * 2 + pair + 1)
                for t in range(2):
                    k = pair * 2 + t
                    last = nc.tensor.matmul(bank[:, t * F * F:(t + 1) * F * F], lhs[:, k * P:(k + 1) * P], rhs,
                                            start=True, stop=True)
                last.then_inc(s_w, 1)

            def produce(n, u, rnd):
                pe.wait_ge(s_g2, n + 1)
                h2_product(n + 1, (u + 1) % 2)
                edge_matrices(n, u, 0, h2[:, u % 2, :], w3[:, :])
                u1 = (u + 2) % U
                h1_product(n + 2, u1, rnd + (u + 2) // U)
                edge_matrices(n, u, 1, h2[:, u % 2, :], w3[:, :])

            def window(g, u, general):
                pe.wait_ge(s_msg, g + 1 + U)
                for k in range(QT):
                    if general:
                        last = nc.tensor.matmul(pwin[u % 2][:, k * R:(k + 1) * R], same[:, u % 2, k, :],
                                                msg[:, u % 2, k, :], start=True, stop=True)
                    else:
                        last = nc.tensor.matmul(pwin[u % 2][0:W, 0:R], hot[:, u % 2, k, :],
                                                msg[:, u % 2, k, :], start=(k == 0), stop=(k == QT - 1))
                last.then_inc(s_win, 1)

            def mix_stage(layer):
                pe.wait_ge(s_nodes, layer + 1)
                for c in range(NC):
                    if c >= 2:
                        pe.wait_ge(s_trc, layer * NC + c - 1)
                    nc.tensor.transpose(pwin[c % 2][0:JB, 0:P],
                                        nodes[:, c * JC:(c + 1) * JC, :].rearrange("p j f -> p (j f)"),
                                        ident[:, :]).then_inc(s_tr, 1)
                    pe.wait_ge(s_trc, layer * NC + c + 1)
                    if c == 0:
                        pe.wait_ge(s_root, layer + 1)
                    if c >= 2:
                        pe.wait_ge(s_mixc, layer * NC + c - 1)
                    nc.tensor.matmul(pmix[c % 2][:, 0:2 * JB], nodeT[:, c % 2, :], mix[:, :],
                                     start=True, stop=True).then_inc(s_mix, 1)
                pe.wait_ge(s_mixc, (layer + 1) * NC)
                pe.nop(nofuse=True)

            pe.wait_ge(s_fit, 1)
            nc.tensor.matmul(pwin[0][:, 0:1], ones[:, :], prep_m[:, 5, 0:1], start=True, stop=True).then_inc(s_fitsum, 1)
            pe.wait_ge(s_at6[0], 16)
            nc.tensor.matmul(ph1[:, :], w1[:, :], at6[:, 0, :], start=True, stop=True).then_inc(s_h1, 1)
            h2_product(0, 0)
            h1_product(1, 1, 0)
            produce(0, 0, 0)
            produce(1, 1, 0)
            pe.wait_ge(s_g1, 4)
            pe.wait_ge(s_g2, 3)
            def layers(general):
                with pe.Fori(0, DEPTH, 1) as layer:
                    mix_stage(layer)
                    with pe.Fori(0, NIT, 1) as it:
                        for u in range(U):
                            g = layer * GL + it * U + u
                            window(g, u, general)
                            v = (u + 2) % U
                            produce(g + 2, v, layer * NIT + it + (u + 2) // U)
                for u in range(2):
                    for pair in range(2):
                        pe.wait_ge(s_at8[u], 16)
                        edge_matrices(LAST * GL + 2 + u, u, pair, at8[:, u, :], wm[:, :])
                with pe.Fori(0, NIT, 1) as it:
                    for u in range(U):
                        g = LAST * GL + it * U + u
                        pe.wait_ge(s_ev, g - 1)
                        window(g, u, general)
                        v = (u + 2) % U
                        pe.wait_ge(s_at8[v], (it + (u + 2) // U + 1) * 16)
                        for pair in range(2):
                            edge_matrices(g + 4, v, pair, at8[:, v, :], wm[:, :])

            pe.wait_ge(s_flag, 1)
            misfits = pe.value_load(flag[0:1, 0:1], min_val=0, max_val=1)
            with pe.If(misfits == 0):
                layers(False)
            with pe.Else():
                layers(True)

        @block.vector
        def _(dve):
            chain = [0]

            def link(ins):
                chain[0] += 1
                ins.then_inc(s_chain, 1)
                dve.wait_ge(s_chain, chain[0])

            dve.sem_inc(s_msg, U)
            dve.sem_inc(s_wfree, 4)
            dve.memset(msg[:, :, :, :], 1.0)
            dve.memset(prep_far[:, :], float(FAR))
            dve.memset(zero[:, :], 0.0).then_inc(s_zsrc, 1)
            dve.wait_ge(s_edge, 32)
            link(nc.vector.tensor_copy(prep_f[:, :, :], prep_dst[:, :, :]))
            nc.vector.tensor_reduce(prep_m[:, 0, :], prep_f[:, :, :], axis=AX.X, op=ALU.min).then_inc(s_dstart, 1)
            nc.vector.tensor_reduce(prep_m[:, 1, :], prep_f[:, :, :], axis=AX.X, op=ALU.max)
            link(nc.vector.tensor_copy(dst_f[:, :], prep_dt))
            dve.wait_ge(s_basefull, 16 * (1 + B))
            nc.vector.tensor_tensor(rel[:, :].rearrange("p (q t) -> p q t", t=QT),
                                    dst_f[:, :].rearrange("p (q t) -> p q t", t=QT),
                                    prep_bb[:, :].unsqueeze(2).to_broadcast([P, NQ, QT]), ALU.subtract)
            nc.vector.tensor_copy(base_i[0:1, :], prep_bb[0:1, :])
            nc.vector.tensor_tensor(prep_m[:, 3, :], prep_m[:, 1, :], prep_m[:, 3, :], ALU.is_ge)
            nc.vector.tensor_tensor(prep_m[:, 2, :], prep_m[:, 1, :], prep_m[:, 2, :], ALU.is_gt)
            link(nc.vector.tensor_tensor(prep_m[:, 4, :], prep_m[:, 1, :], prep_m[:, 0, :], ALU.subtract))
            link(nc.vector.tensor_scalar(prep_m[:, 4, :], prep_m[:, 4, :], float(W), None, ALU.is_ge))
            link(nc.vector.tensor_tensor(prep_m[:, 4, :], prep_m[:, 4, :], prep_m[:, 3, :], ALU.add))
            link(nc.vector.tensor_tensor(prep_m[:, 4, :], prep_m[:, 4, :], prep_m[:, 2, :], ALU.add))
            nc.vector.tensor_reduce(prep_m[:, 5, 0:1], prep_m[:, 4, :], axis=AX.X, op=ALU.add).then_inc(s_fit, 1)
            dve.wait_ge(s_fitsum, 1)
            nc.vector.tensor_scalar(flag[:, :], pwin[0][:, 0:1], 1.0, None, ALU.min).then_inc(s_flag, 1)

            def norm(ready):
                link(nc.vector.tensor_reduce(st[:, 0, :], xs[:, :, :], axis=AX.X, op=ALU.add))
                link(nc.vector.tensor_scalar(st[:, 0, :], st[:, 0, :], 1.0 / F, None, ALU.mult))
                link(nc.vector.tensor_tensor(tmp[:, :, :], xs[:, :, :],
                                             st[:, 0, :].unsqueeze(2).to_broadcast([P, J, F]), ALU.subtract))
                link(nc.vector.tensor_tensor(nodes[:, :, :], tmp[:, :, :], tmp[:, :, :], ALU.mult))
                link(nc.vector.tensor_reduce(st[:, 1, :], nodes[:, :, :], axis=AX.X, op=ALU.add))
                nc.vector.tensor_scalar(st[:, 1, :], st[:, 1, :], 1.0 / F, EPS, ALU.mult, ALU.add).then_inc(s_var, 1)
                dve.wait_ge(s_std, ready)
                link(nc.vector.reciprocal(st[:, 3, :], st[:, 2, :]))
                link(nc.vector.tensor_tensor(nodes[:, :, :], tmp[:, :, :],
                                             st[:, 3, :].unsqueeze(2).to_broadcast([P, J, F]), ALU.mult))

            dve.wait_ge(s_x, 16)
            norm(1)
            nc.vector.tensor_scalar(nodes[:, :, :], nodes[:, :, :], 0.0, None, ALU.max).then_inc(s_nodes, 1)
            dve.wait_ge(s_wt, 16 * (8 + 2 * JC))
            dve.wait_ge(s_const, 5)
            link(nc.vector.memset(first_row[:, :], 0.0))

            def spots(g, q, u):
                c = [0]

                def own(ins):
                    c[0] += 1
                    ins.then_inc(s_gen, 1)
                    dve.wait_ge(s_gen, g * 6 + c[0])
                dst = dst_f[:, bass.ds(q * QT, QT)]
                dve.wait_ge(s_row, g * 16 + 16)
                own(nc.vector.tensor_copy(row_f[:, :, :], row_i[:, :, :]))
                nc.vector.tensor_scalar(spot[:, 3, :], dst, first_row[:, 0:1], None, ALU.add)
                own(nc.vector.tensor_tensor(same[:, u % 2, :, :], row_f[:, :, :],
                                            dst.unsqueeze(2).to_broadcast([P, QT, P]), ALU.is_equal))
                own(nc.vector.tensor_tensor(dup[:, :, :], same[:, u % 2, :, :],
                                            below[:, :].unsqueeze(1).to_broadcast([P, QT, P]), ALU.mult))
                own(nc.vector.tensor_reduce(spot[:, 0, :], dup[:, :, :], axis=AX.X, op=ALU.max))
                own(nc.vector.tensor_scalar(spot[:, 1, :], spot[:, 3, :], spill[:, 0:1], -1.0, ALU.subtract, ALU.mult))
                own(nc.vector.tensor_tensor(spot[:, 2, :], spot[:, 1, :], spot[:, 0, :], ALU.mult))
                nc.vector.tensor_copy(get_i[:, :], spot[:, 3, :])
                nc.vector.tensor_tensor(put_i[:, :], spot[:, 3, :], spot[:, 2, :], ALU.add)

            def quad(g, q, u, rnd, ahead, with_y, general):
                s = u % 2
                dve.wait_ge(s_got[u], (rnd + 1) * 16 * QT)
                for pair in range(2):
                    dve.wait_ge(s_w, (g + ahead) * 2 + pair + 1)
                    nc.vector.tensor_tensor(
                        prod[:, s, pair * 2:pair * 2 + 2, :, :],
                        pw[s * 2 + pair][:, :].rearrange("p (t o i) -> p t o i", t=2, o=F),
                        got[:, u, pair * 2:pair * 2 + 2, F:2 * F].unsqueeze(2).to_broadcast([P, 2, F, F]),
                        ALU.mult).then_inc(s_wfree, 1)
                    if pair == 0 and general:
                        spots(g, q, u)
                    elif pair == 0:
                        nc.vector.tensor_tensor(
                            hot[:, s, :, :], iota[:, :].unsqueeze(1).to_broadcast([P, QT, W]),
                            rel[:, bass.ds(q * QT, QT)].unsqueeze(2).to_broadcast([P, QT, W]), ALU.is_equal)
                dve.wait_ge(s_wfree, (g + ahead) * 2 + 2 + 4)
                red = nc.vector.tensor_reduce(
                    msg[:, s, :, 0:F], prod[:, s, :, :, :].rearrange("p t o i -> p (t o) i"), axis=AX.X, op=ALU.add)
                if with_y:
                    red.then_inc(s_red, 1)
                    dve.wait_ge(s_red, g + 1)
                    nc.vector.tensor_tensor(msg[:, s, :, 0:F], msg[:, s, :, 0:F], got[:, u, :, 0:F],
                                            ALU.add).then_inc(s_msg, 1)
                else:
                    red.then_inc(s_msg, 1)

            def combine(layer):
                c = [0]
                def own(ins):
                    c[0] += 1
                    ins.then_inc(s_comb, 1)
                    dve.wait_ge(s_comb, layer * 5 + c[0])
                dve.wait_ge(s_agg, (layer + 1) * B * 16)
                own(nc.vector.tensor_tensor(agg[:, 0, :], agg[:, 0, :], agg[:, 1, :], ALU.add))
                a = agg[:, 0, :].rearrange("p (j r) -> p j r", r=R)
                return a, own

            def layers(general):
                with dve.Fori(0, DEPTH, 1) as layer:
                    nc.vector.tensor_copy(mix[:, 0:JB], root_all[:, bass.ds(layer, 1), :].rearrange("k a n -> k (a n)")).then_inc(s_root, 1)
                    for c in range(NC):
                        dve.wait_ge(s_mix, layer * NC + c + 1)
                        half = pmix[c % 2][:, 0:2 * JB]
                        nc.vector.tensor_tensor(root[:, c * JC:(c + 1) * JC, :],
                                                half[:, 0:JB].rearrange("p (j f) -> p j f", f=F),
                                                rootb[:, bass.ds(layer, 1), :].to_broadcast([P, JC, F]), ALU.add)
                        nc.vector.tensor_copy(rows[:, c * JC:(c + 1) * JC, 0:F],
                                              half[:, JB:2 * JB].rearrange("p (j f) -> p j f", f=F)).then_inc(s_mixc, 1)
                    nc.vector.tensor_copy(rows[:, :, F:2 * F], nodes[:, :, :]).then_inc(s_rows, 1)
                    with dve.Fori(0, NIT, 1) as it:
                        for u in range(U):
                            q = it * U + u
                            quad(layer * GL + q, q, u, layer * NIT + it, 0, True, general)
                    a, own = combine(layer)
                    deg = a[:, :, F]
                    nc.vector.tensor_scalar(st[:, 1, :], deg, 0.0, None, ALU.is_gt)
                    if general:
                        nc.vector.tensor_scalar(first_row[:, :], first_row[:, :], float(B * NROW), None, ALU.add)
                    own(nc.vector.tensor_scalar(st[:, 0, :], deg, 1.0, None, ALU.max))
                    own(nc.vector.reciprocal(st[:, 2, :], st[:, 0, :]))
                    own(nc.vector.tensor_tensor(st[:, 3, :], st[:, 2, :], st[:, 1, :], ALU.mult))
                    own(nc.vector.tensor_tensor(tmp[:, :, :], a[:, :, 0:F],
                                                st[:, 3, :].unsqueeze(2).to_broadcast([P, J, F]), ALU.mult))
                    nc.vector.tensor_tensor(tmp[:, :, :], tmp[:, :, :], root[:, :, :], ALU.add).then_inc(s_step, 1)
                    dve.wait_ge(s_nodes, layer + 2)
                dve.sem_inc(s_wfree, 4)
                link(nc.vector.tensor_tensor(xs[:, :, :], xs[:, :, :], nodes[:, :, :], ALU.add))
                norm(2)
                nc.vector.tensor_scalar(rows[:, :, F:2 * F], nodes[:, :, :], 0.0, None, ALU.max).then_inc(s_rows, 1)
                with dve.Fori(0, NIT, 1) as it:
                    for u in range(U):
                        q = it * U + u
                        quad(LAST * GL + q, q, u, LAST * NIT + it, 2, False, general)
                a, own = combine(LAST)
                link(nc.vector.tensor_tensor(tmp[:, :, :], a[:, :, 0:F],
                                             outb[:, :].unsqueeze(1).to_broadcast([P, J, F]), ALU.add))
                link(nc.vector.tensor_scalar(tmp[:, :, :], tmp[:, :, :], 0.0, None, ALU.max))
                nc.vector.tensor_tensor(tmp[:, :, :], tmp[:, :, :], xs[:, :, :], ALU.add).then_inc(s_res, 1)

            dve.wait_ge(s_flag, 1)
            misfits = dve.value_load(flag[0:1, 0:1], min_val=0, max_val=1)
            with dve.If(misfits == 0):
                before = chain[0]
                layers(False)
            with dve.Else():
                chain[0] = before
                layers(True)


_OUT = ("out", (NP, F))


def kernel(**inputs):
    import numpy as np
    import concourse.bacc as bacc
    from concourse.bass_utils import run_bass_kernel_spmd

    a = {k: np.ascontiguousarray(v) for k, v in inputs.items()}

    def padded(v, n, fill=0):
        more = np.full((n - v.shape[0],) + v.shape[1:], fill, v.dtype)
        return np.concatenate([v, more])

    def turned(v):
        return np.concatenate([v, v[:U]])

    src = padded(a["src"].astype(np.int32, copy=False), NT * P)
    past = N + np.arange(E, NQP * QE, dtype=np.int32) // QE - E // QE
    dst = np.concatenate([a["dst"].astype(np.int32, copy=False), past.astype(np.int32)])
    src_q = turned(src.reshape(NQ, QT, P).transpose(0, 2, 1)).reshape(-1, QT)

    def attributes(v):
        v = turned(padded(v, NQ * QE).reshape(NQ, QE, -1))
        return v.reshape(-1, v.shape[-1]).T

    arrays = {
        "x": padded(a["x"], NP),
        "src_q": src_q,
        "dst_e": dst.reshape(P, QC, QE),
        "dst_t": dst[:NT * P].reshape(NT, P).T,
        "attr6": attributes(a["edge_attr_6"]),
        "attr8": attributes(a["edge_attr_8"]),
        "kW1": a["L0_gnn_kW1"], "kb1": a["L0_gnn_kb1"],
        "kW2": a["L0_gnn_kW2"], "kb2": a["L0_gnn_kb2"],
        "kW3": a["L0_gnn_kW3"].reshape(KD, F, F).transpose(0, 2, 1).reshape(KD, F * F),
        "kb3": a["L0_gnn_kb3"].reshape(F, F),
        "root_W": a["L0_gnn_root_W"], "root_b": a["L0_gnn_root_b"],
        "Wm": a["L1_gnn_weight_matrix"].reshape(A8, F * F), "bias": a["L1_gnn_bias"],
    }
    arrays = {k: np.ascontiguousarray(v) for k, v in arrays.items()}
    nc = bacc.Bacc("TRN2", target_bir_lowering=False, num_devices=1)
    args = [nc.dram_tensor("in_" + k, v.shape, mybir.dt.from_np(v.dtype), kind="ExternalInput").ap()
            for k, v in arrays.items()]
    args.append(nc.dram_tensor(_OUT[0], _OUT[1], F32, kind="ExternalOutput").ap())
    gnn_program(nc, *args)
    r = run_bass_kernel_spmd(nc, [{"in_" + k: v for k, v in arrays.items()}], core_ids=[0])
    return r.results[0][_OUT[0]][:N]
```

```python
import concourse.bass as bass
from concourse import mybir
from contextlib import ExitStack

N = 12500
E = 412500
F = 16
A6, A8 = 6, 8
A8P = 32
KD = 128
DEPTH = 4
P = 128
J = -(-N // P)
NP = P * J
QT = 4
QE = QT * P
U = 8
NQ = -(-E // QE)
NQ += NQ % 2
NIT, TAIL = divmod(NQ, U)
ROUNDS = [NIT + (u < TAIL) for u in range(U)]
NT = NQ * QT
QC = -(-NQ // P)
NQP = P * QC
W = 32
B = 2
R = F + 1
NROW = NP + P
JC = 7
NC = J // JC
JB = JC * F
RC = 2
RND = NC // RC
SEG = [(0, 4), (4, RND)]
NS = len(SEG)
EPS = 1e-5


def each_quad(engine, body):
    with engine.Fori(0, NIT, 1) as it:
        for u in range(U):
            body(it, u)
    for u in range(TAIL):
        body(NIT, u)


def ahead(layer, it, u, k):
    if it is NIT and u + k >= TAIL:
        v = u + k - TAIL
        return v, (layer + 1) * ROUNDS[v]
    v = (u + k) % U
    return v, layer * ROUNDS[v] + it + (u + k) // U


def columns(seg):
    return slice(SEG[seg][0] * RC * JC, SEG[seg][1] * RC * JC)


FAR = 1 << 20

F32, I32, U32 = mybir.dt.float32, mybir.dt.int32, mybir.dt.uint32
ALU = mybir.AluOpType
ACT = mybir.ActivationFunctionType
AX = mybir.AxisListType


def gnn_program(nc, x, src_q, dst_e, dst_t, attr6, attr8, kW1, kb1, kW2, kb2, kW3, kb3,
                root_W, root_b, Wm, bias, out):
    ctx = ExitStack()
    with ctx:
        def sb(name, shape, dt=F32):
            return ctx.enter_context(nc.sbuf_tensor(name, shape, dt))

        def pb(name, shape):
            return ctx.enter_context(nc.psum_tensor(name, shape, F32))

        def sem(name):
            return ctx.enter_context(nc.semaphore(name))

        table = nc.dram_tensor("table", (NP, 2 * F), F32).ap()
        sums_d = nc.dram_tensor("sums_d", ((DEPTH + 1) * B * NROW, R), F32).ap()
        base_d = nc.dram_tensor("base_d", (NQP + B,), F32).ap()

        w1 = sb("w1", [A6, KD])
        w2 = sb("w2", [KD, KD])
        w3 = sb("w3", [KD, F * F])
        wm = sb("wm", [A8P + A8, F * F])[A8P:A8P + A8, :]
        b1 = sb("b1", [KD, 1])
        b2 = sb("b2", [KD, 1])
        root_all = sb("root_all", [JB + 1, DEPTH, JB])
        mix = sb("mix", [JB + 1, 2 * JB])
        outb = sb("outb", [P, F])
        ident = sb("ident", [P, P])
        iota = sb("iota", [P, W])
        ones = sb("ones", [P, P])
        rel = sb("rel", [P, NT])
        base_i = sb("base_i", [1, NQ], I32)
        flag = sb("flag", [P, 1], I32)
        idx = sb("idx", [P, U, QT], I32)
        attr = sb("attr", [A8P + A8, U, QE])
        at6 = attr[0:A6, :, :]
        at8 = attr[A8P:A8P + A8, :, :]
        got = sb("got", [P, U, QT, 2 * F])
        h1 = sb("h1", [KD, 2, QE])
        h2 = sb("h2", [KD, 2, QE])
        prod = sb("prod", [P, 2, QT, F, F])
        msg = sb("msg", [P, 2, QT, R])
        hot = sb("hot", [P, 2, QT, W])
        sums = sb("sums", [W, 4, R])
        xs = sb("xs", [P, J, F])
        nodes = sb("nodes", [P, J, F])
        root = sb("root", [P, J, F])
        rows = sb("rows", [P, J, 2 * F])
        agg = sb("agg", [P, B, J * R])
        tmp = sb("tmp", [P, J, F])
        st = sb("st", [P, 4, J])
        nodeT = sb("nodeT", [JB + 1, 2, RC * P])
        zero = sb("zero", [P, NROW // P * R])
        spare = agg[:, :, :].rearrange("p k n -> p (k n)").bitcast(I32)
        prep_dt = spare[:, 0:NT]
        prep_dst = sb("prep_dst", [P, QC, QE], I32)
        prep_f = sb("prep_f", [P, QC, QE])
        prep_m = sb("prep_m", [P, 6, QC])
        prep_bb = sb("prep_bb", [P, NQ])
        prep_far = sb("prep_far", [1, B])
        dst_f = sb("dst_f", [P, NT])
        row_i = sb("row_i", [P, QT, P], I32)
        row_f = sb("row_f", [P, QT, P])
        below = sb("below", [P, P])
        same = sb("same", [P, 2, QT, P])
        dup = sb("dup", [P, QT, P])
        spot = sb("spot", [P, 4, QT])
        first_row = sb("first_row", [P, 1])
        spill = sb("spill", [P, 1])
        get_i = sb("get_i", [P, QT], I32)
        put_i = sb("put_i", [P, QT], I32)
        gsum = sb("gsum", [P, 4, QT, R])
        cur = sb("cur", [P, QT, R])

        ph1 = pb("ph1", [P, QE])
        ph2 = pb("ph2", [P, QE])
        pw = [pb(f"pw{b}", [P, QE]) for b in range(4)]
        pwin = [pb(f"pwin{b}", [P, QE]) for b in range(2)]
        pmix = [ph1, ph2]

        s_wt = sem("weights_loaded")
        s_mixw = sem("node_weights_loaded")
        s_ident0 = sem("identity_cleared")
        s_const = sem("constants_made")
        s_clear = sem("block_diagonals_cleared")
        s_edge = sem("edge_places_loaded")
        s_base = sem("bases_stored")
        s_basefull = sem("bases_reloaded")
        s_dstart = sem("quad_base_ready")
        s_fit = sem("misfits_counted")
        s_fitsum = sem("misfits_summed")
        s_flag = sem("flag_ready")
        s_row = sem("dst_row_loaded")
        s_gen = sem("general_step")
        s_cur = sem("general_rows_gathered")
        s_add = sem("general_rows_added")
        s_back = sem("general_rows_scattered")
        s_chain = sem("vector_prep_step")
        s_comb = sem("vector_update_step")
        s_x = sem("x_loaded")
        s_zero = sem("sums_buffers_zeroed")
        s_zsrc = sem("zero_source_made")
        s_idx = [sem(f"idx_loaded{u}") for u in range(U)]
        s_at6 = [sem(f"attr6_loaded{u}") for u in range(U)]
        s_at8 = [sem(f"attr8_loaded{u}") for u in range(U)]
        s_got = [sem(f"rows_gathered{u}") for u in range(U)]
        s_h1 = sem("h1_product_done")
        s_h2 = sem("h2_product_done")
        s_g1 = sem("h1_gelu_done")
        s_g2 = sem("h2_gelu_done")
        s_w = sem("edge_matrices_done")
        s_wfree = sem("edge_matrices_used")
        s_red = sem("products_reduced")
        s_msg = sem("messages_done")
        s_win = sem("window_sums_done")
        s_ev = sem("window_sums_copied")
        s_sfree = sem("window_slots_free")
        s_put = [sem(f"sums_put{m}") for m in range(B)]
        s_agg = [sem(f"sums_loaded{seg}") for seg in range(NS)]
        s_var = sem("variance_ready")
        s_std = sem("deviation_ready")
        s_step = sem("update_input_ready")
        s_nodes = sem("nodes_ready")
        s_root = sem("root_matrix_placed")
        s_res = sem("result_ready")
        s_tr = sem("nodes_transposed")
        s_trc = sem("transpose_copied")
        s_mix = sem("mixed")
        s_mixc = sem("mix_copied")
        s_rows = sem("table_rows_ready")
        s_tab = sem("table_stored")
        s_out = sem("out_stored")

        block = ctx.enter_context(nc.Block())

        table_p = table.rearrange("(p j) f -> p j f", p=P)
        x_p = x.rearrange("(p j) f -> p j f", p=P)
        out_p = out.rearrange("(p j) f -> p j f", p=P)
        GL = NQ
        LAST = DEPTH

        def sums_rows(layer, m, n):
            return sums_d[bass.ds((layer * B + m) * NROW, n), :].rearrange("(p j) r -> p (j r)", p=P)

        @block.sync
        def _(sp):
            sp.dma_start(xs[:, :, :], x_p).then_inc(s_x, 16)
            sp.dma_start(prep_dst[:, :, :], dst_e).then_inc(s_edge, 16)
            sp.dma_start(prep_dt, dst_t).then_inc(s_edge, 16)
            sp.wait_ge(s_dstart, 1)
            sp.dma_start(base_d[0:NQP].rearrange("(p c) -> p c", p=P), prep_m[:, 0, :]).then_inc(s_base, 16)
            sp.dma_start(base_d[NQP:NQP + B].rearrange("(a n) -> a n", a=1), prep_far[0:1, :]).then_inc(s_base, 16)
            sp.wait_ge(s_base, 32)
            sp.dma_start(prep_bb[:, :], base_d[0:NQ].rearrange("(a n) -> a n", a=1).to_broadcast([P, NQ])
                         ).then_inc(s_basefull, 16)
            for m in range(B):
                sp.dma_start(prep_m[:, 2 + m, :], base_d[1 + m:1 + m + NQP].rearrange("(p c) -> p c", p=P)
                             ).then_inc(s_basefull, 16)
            sp.wait_ge(s_zsrc, 1)
            for m in range(B):
                sp.dma_start(sums_rows(0, m, NROW), zero[:, :]).then_inc(s_put[m], 16)

            def zeros(layer):
                for m in range(B):
                    sp.dma_start(sums_rows(layer, m, NROW), zero[:, :]).then_inc(s_zero, 16)

            def place_windows(layer):
                def place(it, u):
                    q = it * U + u
                    g = layer * GL + q
                    m = u % B
                    base = sp.value_load(base_i[0:1, bass.ds(q, 1)], min_val=0, max_val=NP - W)
                    sp.wait_ge(s_ev, g + 1)
                    sp.wait_ge(s_put[m], (layer * (GL // B) + it * (U // B) + (u // B + 1)) * 16)
                    sp.dma_start(sums_d[bass.ds(base + (layer * B + m) * NROW, W), :],
                                 sums[:, u % 4, :]).then_inc(s_put[m], 16)
                    sp.sem_inc(s_sfree, 1)
                each_quad(sp, place)

            def dst_rows(layer):
                def dst_row(it, u):
                    g = layer * GL + it * U + u
                    sp.wait_ge(s_msg, g + U)
                    sp.dma_start(row_i[:, :, :].rearrange("p t e -> p (t e)"),
                                 dst_e.rearrange("p c e -> (p c) e")[bass.ds(it * U + u, 1), :].to_broadcast([P, QE])
                                 ).then_inc(s_row, 16)
                each_quad(sp, dst_row)

            def load_sums(layer, general):
                if general:
                    sp.wait_ge(s_back, (layer + 1) * (GL * QT * 16))
                    sp.wait_ge(s_put[1], 16)
                else:
                    for m in range(B):
                        sp.wait_ge(s_put[m], ((layer + 1) * (GL // B) + 1) * 16)
                for seg in range(NS):
                    c = columns(seg)
                    for m in range(B):
                        sp.dma_start(agg[:, m, c.start * R:c.stop * R],
                                     sums_rows(layer, m, NP)[:, c.start * R:c.stop * R]).then_inc(s_agg[seg], 16)

            def layers(general):
                add_up = dst_rows if general else place_windows
                with sp.Fori(0, DEPTH, 1) as layer:
                    for seg in range(NS):
                        sp.wait_ge(s_mixc, layer * RND + SEG[seg][1])
                        sp.dma_start(table_p[:, columns(seg), :], rows[:, columns(seg), :]).then_inc(s_tab, 16)
                    if not general:
                        zeros(layer + 1)
                    add_up(layer)
                    sp.wait_ge(s_zero, (layer + 1) * B * 16)
                    sp.nop(nofuse=True)
                    load_sums(layer, general)
                sp.wait_ge(s_rows, 1)
                sp.dma_start(table_p, rows[:, :, :]).then_inc(s_tab, 16)
                add_up(LAST)
                load_sums(LAST, general)

            sp.wait_ge(s_flag, 1)
            misfits = sp.value_load(flag[0:1, 0:1], min_val=0, max_val=1)
            with sp.If(misfits == 0):
                layers(False)
            with sp.Else():
                for layer in range(1, DEPTH + 1):
                    zeros(layer)
                layers(True)
            for seg in range(NS):
                sp.wait_ge(s_res, seg + 1)
                sp.dma_start(out_p[:, columns(seg), :], tmp[:, columns(seg), :]).then_inc(s_out, 16)
            sp.wait_ge(s_out, 16 * NS)

        @block.gpsimd
        def _(pool):
            pool.memset(ident[:, :], 0.0).then_inc(s_ident0, 1)
            pool.memset(root_all[:, :, :], 0.0).then_inc(s_clear, 1)
            pool.memset(mix[:, :], 0.0).then_inc(s_clear, 1)
            pool.iota(iota[:, :], pattern=[[1, W]], base=0, channel_multiplier=0,
                      allow_small_or_imprecise_dtypes=True).then_inc(s_const, 1)
            pool.wait_ge(s_ident0, 1)
            pool.affine_select(out=ident[:, :], in_=ident[:, :], compare_op=ALU.not_equal, fill=1.0,
                               base=0, pattern=[[-1, P]], channel_multiplier=1).then_inc(s_const, 1)

            pool.memset(ones[:, :], 1.0).then_inc(s_const, 1)
            pool.memset(below[:, :], 1.0).then_inc(s_ident0, 1)
            pool.wait_ge(s_ident0, 2)
            pool.affine_select(out=below[:, :], in_=below[:, :], compare_op=ALU.is_ge, fill=0.0,
                               base=-1, pattern=[[-1, P]], channel_multiplier=1).then_inc(s_const, 1)
            pool.iota(spill[:, :], pattern=[[1, 1]], base=NP, channel_multiplier=1,
                      allow_small_or_imprecise_dtypes=True).then_inc(s_const, 1)

            def add_rows(g, u):
                pool.wait_ge(s_ev, g + 1)
                for k in range(QT):
                    n = g * QT + k
                    pool.nop(nofuse=True)
                    pool.indirect_dma_start(
                        cur[:, k, :], None, sums_d[:, :],
                        bass.IndirectOffsetOnAxis(ap=get_i[:, k:k + 1].bitcast(U32), axis=0)).then_inc(s_cur, 16)
                    pool.wait_ge(s_cur, n * 16 + 16)
                    pool.tensor_tensor(cur[:, k, :], cur[:, k, :], gsum[:, u % 4, k, :], ALU.add).then_inc(s_add, 1)
                    pool.wait_ge(s_add, n + 1)
                    pool.nop(nofuse=True)
                    pool.indirect_dma_start(
                        sums_d[:, :], bass.IndirectOffsetOnAxis(ap=put_i[:, k:k + 1].bitcast(U32), axis=0),
                        cur[:, k, :], None).then_inc(s_back, 16)
                    pool.wait_ge(s_back, n * 16 + 16)
                pool.sem_inc(s_sfree, 1)

            def layer_gathers(layer, general):
                pool.wait_ge(s_tab, DEPTH * NS * 16 + 16 if layer is LAST else (layer + 1) * NS * 16)
                pool.nop(nofuse=True)
                def gathers(it, u):
                    g = layer * GL + it * U + u
                    pool.wait_ge(s_idx[u], (layer * ROUNDS[u] + it + 1) * 16)
                    pool.wait_ge(s_msg, g + 1)
                    pool.nop(nofuse=True)
                    for k in range(QT):
                        pool.indirect_dma_start(
                            got[:, u, k, :], None, table[:, :],
                            bass.IndirectOffsetOnAxis(ap=idx[:, u, k:k + 1].bitcast(U32), axis=0),
                        ).then_inc(s_got[u], 16)
                    if general:
                        add_rows(g, u)
                each_quad(pool, gathers)

            def layers(general):
                with pool.Fori(0, DEPTH, 1) as layer:
                    layer_gathers(layer, general)
                layer_gathers(LAST, general)

            pool.wait_ge(s_flag, 1)
            misfits = pool.value_load(flag[0:1, 0:1], min_val=0, max_val=1)
            with pool.If(misfits == 0):
                layers(False)
            with pool.Else():
                for m in range(B):
                    pool.wait_ge(s_put[m], 16)
                pool.wait_ge(s_zero, DEPTH * B * 16)
                layers(True)

        @block.scalar
        def _(act):
            act.dma_start(b1[:, :], kb1.rearrange("(k a) -> k a", a=1)).then_inc(s_wt, 16)
            act.dma_start(b2[:, :], kb2.rearrange("(k a) -> k a", a=1)).then_inc(s_wt, 16)
            for dst, srcw in ((w1, kW1), (w2, kW2), (w3, kW3)):
                act.dma_start(dst[:, :], srcw).then_inc(s_wt, 16)

            def load_edges(u, q, attr, ring, ring_sem):
                act.dma_start(idx[:, u, :], src_q[bass.ds(q * P, P), :]).then_inc(s_idx[u], 16)
                act.dma_start(ring[:, u, :], attr[:, bass.ds(q * QE, QE)]).then_inc(ring_sem[u], 16)

            for u in range(U):
                load_edges(u, u, attr6, at6, s_at6)
            act.wait_ge(s_clear, 2)
            for c in range(JC):
                act.dma_start(root_all[c * F:(c + 1) * F, :, c * F:(c + 1) * F],
                              root_W.rearrange("d i o -> i d o")).then_inc(s_mixw, 16)
                act.dma_start(mix[c * F:(c + 1) * F, JB + c * F:JB + (c + 1) * F], kb3).then_inc(s_mixw, 16)
                act.dma_start(root_all[JB:JB + 1, :, c * F:(c + 1) * F],
                              root_b.rearrange("(a d) f -> a d f", a=1)).then_inc(s_mixw, 16)
            act.dma_start(wm[:, :], Wm).then_inc(s_mixw, 16)
            act.dma_start(outb[:, :], bias.rearrange("(a f) -> a f", a=1).to_broadcast([P, F])).then_inc(s_mixw, 16)
            act.sem_inc(s_sfree, 2)
            act.wait_ge(s_wt, 16 * 5)

            def gelu1(n, par):
                act.wait_ge(s_h1, n + 1)
                nc.scalar.activation(h1[:, par, :], ph1[:, :], ACT.Gelu_apprx_tanh, bias=b1[:, 0:1]).then_inc(s_g1, 1)

            def gelu2(n, par):
                act.wait_ge(s_h2, n + 1)
                nc.scalar.activation(h2[:, par, :], ph2[:, :], ACT.Gelu_apprx_tanh, bias=b2[:, 0:1]).then_inc(s_g2, 1)

            def window(g, u, general):
                act.wait_ge(s_win, g + 1)
                act.wait_ge(s_sfree, g + 1)
                if general:
                    nc.scalar.copy(gsum[:, u % 4, :, :],
                                   pwin[u % 2][:, 0:QT * R].rearrange("p (k r) -> p k r", k=QT)).then_inc(s_ev, 1)
                else:
                    nc.scalar.copy(sums[:, u % 4, :], pwin[u % 2][0:W, 0:R]).then_inc(s_ev, 1)

            def deviation(count):
                act.wait_ge(s_var, count)
                nc.scalar.activation(st[:, 2, :], st[:, 1, :], ACT.Sqrt).then_inc(s_std, 1)

            deviation(1)

            def mix_stage(count):
                for r in range(RND):
                    act.wait_ge(s_tr, count + r + 1)
                    nc.scalar.copy(nodeT[0:JB, r % 2, :], pwin[r % 2][0:JB, 0:RC * P]).then_inc(s_trc, 1)

            gelu1(0, 0)
            gelu2(0, 0)
            gelu1(1, 1)
            gelu2(1, 1)
            gelu1(2, 0)
            gelu2(2, 0)
            gelu1(3, 1)
            def layers(general):
                with act.Fori(0, DEPTH, 1) as layer:
                    mix_stage(layer * RND)
                    def hidden(it, u):
                        g = layer * GL + it * U + u
                        window(g, u, general)
                        load_edges(u, it * U + u + U, attr6, at6, s_at6)
                        gelu2(g + 3, (u + 3) % 2)
                        gelu1(g + 4, (u + 4) % 2)
                    each_quad(act, hidden)
                    for seg in range(NS):
                        act.wait_ge(s_step, layer * NS + seg + 1)
                        nc.scalar.activation(nodes[:, columns(seg), :], tmp[:, columns(seg), :],
                                             ACT.Gelu_apprx_tanh).then_inc(s_nodes, 1)
                for u in range(U):
                    act.dma_start(at8[:, u, :], attr8[:, u * QE:(u + 1) * QE]).then_inc(s_at8[u], 16)
                deviation(2)
                def last_layer(it, u):
                    window(LAST * GL + it * U + u, u, general)
                    load_edges(u, it * U + u + U, attr8, at8, s_at8)
                each_quad(act, last_layer)

            act.wait_ge(s_flag, 1)
            misfits = act.value_load(flag[0:1, 0:1], min_val=0, max_val=1)
            with act.If(misfits == 0):
                layers(False)
            with act.Else():
                layers(True)
            for u in range(U):
                act.wait_ge(s_idx[u], 16 * ((DEPTH + 1) * ROUNDS[u] + 1))
                act.wait_ge(s_at6[u], 16 * (DEPTH * ROUNDS[u] + 1))
                act.wait_ge(s_at8[u], 16 * (ROUNDS[u] + 1))

        @block.tensor
        def _(pe):
            pe.wait_ge(s_wt, 16 * 5)

            def h1_product(n, u, rnd):
                pe.wait_ge(s_at6[u], (rnd + 1) * 16)
                pe.wait_ge(s_g1, n)
                nc.tensor.matmul(ph1[:, :], w1[:, :], at6[:, u, :], start=True, stop=True).then_inc(s_h1, 1)

            def h2_product(n, par):
                pe.wait_ge(s_g1, n + 1)
                nc.tensor.matmul(ph2[:, :], w2[:, :], h1[:, par, :], start=True, stop=True).then_inc(s_h2, 1)

            def edge_matrices(n, u, pair, lhs, rhs):
                bank = pw[u % 2 * 2 + pair]
                pe.wait_ge(s_wfree, n * 2 + pair + 1)
                for t in range(2):
                    k = pair * 2 + t
                    last = nc.tensor.matmul(bank[:, t * F * F:(t + 1) * F * F], lhs[:, k * P:(k + 1) * P], rhs,
                                            start=True, stop=True)
                last.then_inc(s_w, 1)

            def produce(n, u, u1, rnd1):
                pe.wait_ge(s_g2, n + 1)
                h2_product(n + 1, (u + 1) % 2)
                edge_matrices(n, u, 0, h2[:, u % 2, :], w3[:, :])
                h1_product(n + 2, u1, rnd1)
                edge_matrices(n, u, 1, h2[:, u % 2, :], w3[:, :])

            def window(g, u, general):
                pe.wait_ge(s_msg, g + 1 + U)
                for k in range(QT):
                    if general:
                        last = nc.tensor.matmul(pwin[u % 2][:, k * R:(k + 1) * R], same[:, u % 2, k, :],
                                                msg[:, u % 2, k, :], start=True, stop=True)
                    else:
                        last = nc.tensor.matmul(pwin[u % 2][0:W, 0:R], hot[:, u % 2, k, :],
                                                msg[:, u % 2, k, :], start=(k == 0), stop=(k == QT - 1))
                last.then_inc(s_win, 1)

            def mix_stage(layer):
                pe.wait_ge(s_nodes, (layer + 1) * NS)

                def transposes(r):
                    if r >= 2:
                        pe.wait_ge(s_trc, layer * RND + r - 1)
                    for t in range(RC):
                        c = r * RC + t
                        last = nc.tensor.transpose(pwin[r % 2][0:JB, t * P:(t + 1) * P],
                                                   nodes[:, c * JC:(c + 1) * JC, :].rearrange("p j f -> p (j f)"),
                                                   ident[:, :])
                    last.then_inc(s_tr, 1)

                transposes(0)
                pe.wait_ge(s_root, layer + 1)
                for r in range(RND):
                    if r + 1 < RND:
                        transposes(r + 1)
                    pe.wait_ge(s_trc, layer * RND + r + 1)
                    if r >= 2:
                        pe.wait_ge(s_mixc, layer * RND + r - 1)
                    for t in range(RC):
                        last = nc.tensor.matmul(pmix[r % 2][:, t * 2 * JB:(t + 1) * 2 * JB],
                                                nodeT[:, r % 2, t * P:(t + 1) * P], mix[:, :], start=True, stop=True)
                    last.then_inc(s_mix, 1)
                pe.wait_ge(s_mixc, (layer + 1) * RND)
                pe.nop(nofuse=True)

            pe.wait_ge(s_at6[0], 16)
            nc.tensor.matmul(ph1[:, :], w1[:, :], at6[:, 0, :], start=True, stop=True).then_inc(s_h1, 1)
            h2_product(0, 0)
            h1_product(1, 1, 0)
            pe.wait_ge(s_const, 5)
            pe.wait_ge(s_fit, 1)
            nc.tensor.matmul(pwin[0][:, 0:1], ones[:, :], prep_m[:, 5, 0:1], start=True, stop=True).then_inc(s_fitsum, 1)
            produce(0, 0, 2, 0)
            produce(1, 1, 3, 0)
            pe.wait_ge(s_mixw, 16 * (3 * JC + 2))
            pe.wait_ge(s_g1, 4)
            pe.wait_ge(s_g2, 3)
            def layers(general):
                with pe.Fori(0, DEPTH, 1) as layer:
                    mix_stage(layer)
                    def products(it, u):
                        g = layer * GL + it * U + u
                        window(g, u, general)
                        produce(g + 2, ahead(layer, it, u, 2)[0], *ahead(layer, it, u, 4))
                    each_quad(pe, products)
                for u in range(2):
                    for pair in range(2):
                        pe.wait_ge(s_at8[u], 16)
                        edge_matrices(LAST * GL + 2 + u, u, pair, at8[:, u, :], wm[:, :])
                def last_products(it, u):
                    g = LAST * GL + it * U + u
                    pe.wait_ge(s_ev, g - 1)
                    window(g, u, general)
                    v, rnd = ahead(0, it, u, 2)
                    pe.wait_ge(s_at8[v], (rnd + 1) * 16)
                    for pair in range(2):
                        edge_matrices(g + 4, v, pair, at8[:, v, :], wm[:, :])
                each_quad(pe, last_products)

            pe.wait_ge(s_flag, 1)
            misfits = pe.value_load(flag[0:1, 0:1], min_val=0, max_val=1)
            with pe.If(misfits == 0):
                layers(False)
            with pe.Else():
                layers(True)

        @block.vector
        def _(dve):
            chain = [0]

            def link(ins):
                chain[0] += 1
                ins.then_inc(s_chain, 1)
                dve.wait_ge(s_chain, chain[0])

            dve.sem_inc(s_msg, U)
            dve.sem_inc(s_wfree, 4)
            dve.memset(msg[:, :, :, :], 1.0)
            def norm(ready):
                link(nc.vector.tensor_reduce(st[:, 0, :], xs[:, :, :], axis=AX.X, op=ALU.add))
                link(nc.vector.tensor_scalar(st[:, 0, :], st[:, 0, :], 1.0 / F, None, ALU.mult))
                link(nc.vector.tensor_tensor(tmp[:, :, :], xs[:, :, :],
                                             st[:, 0, :].unsqueeze(2).to_broadcast([P, J, F]), ALU.subtract))
                link(nc.vector.tensor_tensor(nodes[:, :, :], tmp[:, :, :], tmp[:, :, :], ALU.mult))
                link(nc.vector.tensor_reduce(st[:, 1, :], nodes[:, :, :], axis=AX.X, op=ALU.add))
                nc.vector.tensor_scalar(st[:, 1, :], st[:, 1, :], 1.0 / F, EPS, ALU.mult, ALU.add).then_inc(s_var, 1)
                dve.wait_ge(s_std, ready)
                link(nc.vector.reciprocal(st[:, 3, :], st[:, 2, :]))
                link(nc.vector.tensor_tensor(nodes[:, :, :], tmp[:, :, :],
                                             st[:, 3, :].unsqueeze(2).to_broadcast([P, J, F]), ALU.mult))

            dve.memset(prep_far[:, :], float(FAR))
            dve.wait_ge(s_edge, 32)
            link(nc.vector.tensor_copy(prep_f[:, :, :], prep_dst[:, :, :]))
            nc.vector.tensor_reduce(prep_m[:, 0, :], prep_f[:, :, :], axis=AX.X, op=ALU.min).then_inc(s_dstart, 1)
            dve.memset(zero[:, :], 0.0).then_inc(s_zsrc, 1)
            dve.memset(nodeT[:, :, :], 1.0)

            dve.wait_ge(s_x, 16)
            norm(1)
            for seg in range(NS):
                nc.vector.tensor_scalar(nodes[:, columns(seg), :], nodes[:, columns(seg), :], 0.0, None,
                                        ALU.max).then_inc(s_nodes, 1)
            nc.vector.tensor_reduce(prep_m[:, 1, :], prep_f[:, :, :], axis=AX.X, op=ALU.max)
            link(nc.vector.tensor_copy(dst_f[:, :], prep_dt))
            dve.wait_ge(s_basefull, 16 * (1 + B))
            nc.vector.tensor_tensor(rel[:, :].rearrange("p (q t) -> p q t", t=QT),
                                    dst_f[:, :].rearrange("p (q t) -> p q t", t=QT),
                                    prep_bb[:, :].unsqueeze(2).to_broadcast([P, NQ, QT]), ALU.subtract)
            nc.vector.tensor_copy(base_i[0:1, :], prep_bb[0:1, :])
            nc.vector.tensor_tensor(prep_m[:, 3, :], prep_m[:, 1, :], prep_m[:, 3, :], ALU.is_ge)
            nc.vector.tensor_tensor(prep_m[:, 2, :], prep_m[:, 1, :], prep_m[:, 2, :], ALU.is_gt)
            link(nc.vector.tensor_tensor(prep_m[:, 4, :], prep_m[:, 1, :], prep_m[:, 0, :], ALU.subtract))
            link(nc.vector.tensor_scalar(prep_m[:, 4, :], prep_m[:, 4, :], float(W), None, ALU.is_ge))
            link(nc.vector.tensor_tensor(prep_m[:, 4, :], prep_m[:, 4, :], prep_m[:, 3, :], ALU.add))
            link(nc.vector.tensor_tensor(prep_m[:, 4, :], prep_m[:, 4, :], prep_m[:, 2, :], ALU.add))
            nc.vector.tensor_reduce(prep_m[:, 5, 0:1], prep_m[:, 4, :], axis=AX.X, op=ALU.add).then_inc(s_fit, 1)
            dve.wait_ge(s_fitsum, 1)
            nc.vector.tensor_scalar(flag[:, :], pwin[0][:, 0:1], 1.0, None, ALU.min).then_inc(s_flag, 1)

            dve.wait_ge(s_mixw, 16 * (3 * JC + 2))
            dve.wait_ge(s_const, 5)
            link(nc.vector.memset(first_row[:, :], 0.0))

            def spots(g, q, u):
                c = [0]

                def own(ins):
                    c[0] += 1
                    ins.then_inc(s_gen, 1)
                    dve.wait_ge(s_gen, g * 6 + c[0])
                dst = dst_f[:, bass.ds(q * QT, QT)]
                dve.wait_ge(s_row, g * 16 + 16)
                own(nc.vector.tensor_copy(row_f[:, :, :], row_i[:, :, :]))
                nc.vector.tensor_scalar(spot[:, 3, :], dst, first_row[:, 0:1], None, ALU.add)
                own(nc.vector.tensor_tensor(same[:, u % 2, :, :], row_f[:, :, :],
                                            dst.unsqueeze(2).to_broadcast([P, QT, P]), ALU.is_equal))
                own(nc.vector.tensor_tensor(dup[:, :, :], same[:, u % 2, :, :],
                                            below[:, :].unsqueeze(1).to_broadcast([P, QT, P]), ALU.mult))
                own(nc.vector.tensor_reduce(spot[:, 0, :], dup[:, :, :], axis=AX.X, op=ALU.max))
                own(nc.vector.tensor_scalar(spot[:, 1, :], spot[:, 3, :], spill[:, 0:1], -1.0, ALU.subtract, ALU.mult))
                own(nc.vector.tensor_tensor(spot[:, 2, :], spot[:, 1, :], spot[:, 0, :], ALU.mult))
                nc.vector.tensor_copy(get_i[:, :], spot[:, 3, :])
                nc.vector.tensor_tensor(put_i[:, :], spot[:, 3, :], spot[:, 2, :], ALU.add)

            def quad(g, q, u, rnd, ahead, with_y, general):
                s = u % 2
                dve.wait_ge(s_got[u], (rnd + 1) * 16 * QT)
                for pair in range(2):
                    dve.wait_ge(s_w, (g + ahead) * 2 + pair + 1)
                    nc.vector.tensor_tensor(
                        prod[:, s, pair * 2:pair * 2 + 2, :, :],
                        pw[s * 2 + pair][:, :].rearrange("p (t o i) -> p t o i", t=2, o=F),
                        got[:, u, pair * 2:pair * 2 + 2, F:2 * F].unsqueeze(2).to_broadcast([P, 2, F, F]),
                        ALU.mult).then_inc(s_wfree, 1)
                    if pair == 0 and general:
                        spots(g, q, u)
                    elif pair == 0:
                        nc.vector.tensor_tensor(
                            hot[:, s, :, :], iota[:, :].unsqueeze(1).to_broadcast([P, QT, W]),
                            rel[:, bass.ds(q * QT, QT)].unsqueeze(2).to_broadcast([P, QT, W]), ALU.is_equal)
                dve.wait_ge(s_wfree, (g + ahead) * 2 + 2 + 4)
                red = nc.vector.tensor_reduce(
                    msg[:, s, :, 0:F], prod[:, s, :, :, :].rearrange("p t o i -> p (t o) i"), axis=AX.X, op=ALU.add)
                if with_y:
                    red.then_inc(s_red, 1)
                    dve.wait_ge(s_red, g + 1)
                    nc.vector.tensor_tensor(msg[:, s, :, 0:F], msg[:, s, :, 0:F], got[:, u, :, 0:F],
                                            ALU.add).then_inc(s_msg, 1)
                else:
                    red.then_inc(s_msg, 1)

            def combine(layer):
                c = [0]
                def own(ins):
                    c[0] += 1
                    ins.then_inc(s_comb, 1)
                    dve.wait_ge(s_comb, layer * (5 * NS) + c[0])
                def part(seg):
                    dve.wait_ge(s_agg[seg], (layer + 1) * B * 16)
                    c = columns(seg)
                    both = agg[:, :, c.start * R:c.stop * R]
                    own(nc.vector.tensor_tensor(both[:, 0, :], both[:, 0, :], both[:, 1, :], ALU.add))
                    return both[:, 0, :].rearrange("p (j r) -> p j r", r=R)
                return part, own

            def layers(general):
                with dve.Fori(0, DEPTH, 1) as layer:
                    nc.vector.tensor_copy(mix[:, 0:JB], root_all[:, bass.ds(layer, 1), :].rearrange("k a n -> k (a n)")).then_inc(s_root, 1)
                    dve.wait_ge(s_nodes, (layer + 1) * NS)
                    nc.vector.tensor_copy(rows[:, :, F:2 * F], nodes[:, :, :])
                    for r in range(RND):
                        c = slice(r * RC * JC, (r + 1) * RC * JC)
                        dve.wait_ge(s_mix, layer * RND + r + 1)
                        out4 = pmix[r % 2][:, 0:RC * 2 * JB].rearrange("p (t h j f) -> p t h j f", t=RC, h=2, f=F)
                        nc.vector.tensor_copy(rows[:, c, 0:F].rearrange("p (t j) f -> p t j f", t=RC), out4[:, :, 1])
                        nc.vector.tensor_copy(root[:, c, :].rearrange("p (t j) f -> p t j f", t=RC),
                                              out4[:, :, 0]).then_inc(s_mixc, 1)
                    def messages(it, u):
                        q = it * U + u
                        quad(layer * GL + q, q, u, layer * ROUNDS[u] + it, 0, True, general)
                    each_quad(dve, messages)
                    part, own = combine(layer)
                    if general:
                        nc.vector.tensor_scalar(first_row[:, :], first_row[:, :], float(B * NROW), None, ALU.add)
                    for seg in range(NS):
                        c = columns(seg)
                        a = part(seg)
                        nc.vector.tensor_scalar(st[:, 1, c], a[:, :, F], 0.0, None, ALU.is_gt)
                        own(nc.vector.tensor_scalar(st[:, 0, c], a[:, :, F], 1.0, None, ALU.max))
                        own(nc.vector.reciprocal(st[:, 2, c], st[:, 0, c]))
                        own(nc.vector.tensor_tensor(st[:, 3, c], st[:, 2, c], st[:, 1, c], ALU.mult))
                        own(nc.vector.tensor_tensor(tmp[:, c, :], a[:, :, 0:F],
                                                    st[:, 3, c].unsqueeze(2).to_broadcast([P, c.stop - c.start, F]),
                                                    ALU.mult))
                        nc.vector.tensor_tensor(tmp[:, c, :], tmp[:, c, :], root[:, c, :], ALU.add).then_inc(s_step, 1)
                dve.wait_ge(s_nodes, (DEPTH + 1) * NS)
                dve.sem_inc(s_wfree, 4)
                link(nc.vector.tensor_tensor(xs[:, :, :], xs[:, :, :], nodes[:, :, :], ALU.add))
                norm(2)
                nc.vector.tensor_scalar(rows[:, :, F:2 * F], nodes[:, :, :], 0.0, None, ALU.max).then_inc(s_rows, 1)
                def last_messages(it, u):
                    q = it * U + u
                    quad(LAST * GL + q, q, u, LAST * ROUNDS[u] + it, 2, False, general)
                each_quad(dve, last_messages)
                part, own = combine(LAST)
                for seg in range(NS):
                    c = columns(seg)
                    a = part(seg)
                    link(nc.vector.tensor_tensor(tmp[:, c, :], a[:, :, 0:F],
                                                 outb[:, :].unsqueeze(1).to_broadcast([P, c.stop - c.start, F]), ALU.add))
                    link(nc.vector.tensor_scalar(tmp[:, c, :], tmp[:, c, :], 0.0, None, ALU.max))
                    nc.vector.tensor_tensor(tmp[:, c, :], tmp[:, c, :], xs[:, c, :], ALU.add).then_inc(s_res, 1)

            dve.wait_ge(s_flag, 1)
            misfits = dve.value_load(flag[0:1, 0:1], min_val=0, max_val=1)
            with dve.If(misfits == 0):
                before = chain[0]
                layers(False)
            with dve.Else():
                chain[0] = before
                layers(True)


_OUT = ("out", (NP, F))


def kernel(**inputs):
    import numpy as np
    import concourse.bacc as bacc
    from concourse.bass_utils import run_bass_kernel_spmd

    a = {k: np.ascontiguousarray(v) for k, v in inputs.items()}

    def padded(v, n, fill=0):
        more = np.full((n - v.shape[0],) + v.shape[1:], fill, v.dtype)
        return np.concatenate([v, more])

    def turned(v):
        return np.concatenate([v, v[TAIL:U], v[:TAIL]])

    src = padded(a["src"].astype(np.int32, copy=False), NT * P)
    past = N + np.arange(E, NQP * QE, dtype=np.int32) // QE - E // QE
    dst = np.concatenate([a["dst"].astype(np.int32, copy=False), past.astype(np.int32)])
    src_q = turned(src.reshape(NQ, QT, P).transpose(0, 2, 1)).reshape(-1, QT)

    def attributes(v):
        v = turned(padded(v, NQ * QE).reshape(NQ, QE, -1))
        return v.reshape(-1, v.shape[-1]).T

    arrays = {
        "x": padded(a["x"], NP),
        "src_q": src_q,
        "dst_e": dst.reshape(P, QC, QE),
        "dst_t": dst[:NT * P].reshape(NT, P).T,
        "attr6": attributes(a["edge_attr_6"]),
        "attr8": attributes(a["edge_attr_8"]),
        "kW1": a["L0_gnn_kW1"], "kb1": a["L0_gnn_kb1"],
        "kW2": a["L0_gnn_kW2"], "kb2": a["L0_gnn_kb2"],
        "kW3": a["L0_gnn_kW3"].reshape(KD, F, F).transpose(0, 2, 1).reshape(KD, F * F),
        "kb3": a["L0_gnn_kb3"].reshape(F, F),
        "root_W": a["L0_gnn_root_W"], "root_b": a["L0_gnn_root_b"],
        "Wm": a["L1_gnn_weight_matrix"].reshape(A8, F * F), "bias": a["L1_gnn_bias"],
    }
    arrays = {k: np.ascontiguousarray(v) for k, v in arrays.items()}
    nc = bacc.Bacc("TRN2", target_bir_lowering=False, num_devices=1)
    args = [nc.dram_tensor("in_" + k, v.shape, mybir.dt.from_np(v.dtype), kind="ExternalInput").ap()
            for k, v in arrays.items()]
    args.append(nc.dram_tensor(_OUT[0], _OUT[1], F32, kind="ExternalOutput").ap())
    gnn_program(nc, *args)
    r = run_bass_kernel_spmd(nc, [{"in_" + k: v for k, v in arrays.items()}], core_ids=[0])
    return r.results[0][_OUT[0]][:N]
```
